# Optimizing a Trainium2 kernel written in Bass

```python
import numpy as np
import jax
import jax.numpy as jnp

def _softmax(x, axis=-1):
    return jax.nn.softmax(x, axis=axis)

def _gelu(x):
    return jax.nn.gelu(x, approximate=True)

def _silu(x):
    return jax.nn.silu(x)

def _sigmoid(x):
    return jax.nn.sigmoid(x)

def _layernorm(x, axis=-1, eps=1e-05):
    m = jnp.mean(x, axis=axis, keepdims=True)
    v = jnp.var(x, axis=axis, keepdims=True)
    return (x - m) / jnp.sqrt(v + eps)

def _scatter_add(tgt, idx, src, axis=0):
    return tgt.at[idx].add(src)

def _segment_sum(src, seg, n):
    return jax.ops.segment_sum(src, seg, n)
kernel_name = 'mk_recurrent_d1_jaxref_r8_94417e'

def setup_inputs(seed: int=0):
    np.random.seed(seed)
    _w = jnp.asarray

    def _L0_attn_setup():
        import jax, jax.numpy as jnp
        import numpy as np
        EPS = 1e-05

        def xpos_rotate(x, offset=0, conjugate=False):
            b, s, h, dh = x.shape
            expoent = jnp.arange(0, dh, 2, dtype=jnp.float32) / dh
            angle = 10.0 ** (-4.0 * expoent)
            if conjugate:
                angle = -angle
            pos = jnp.arange(offset, s + offset, dtype=jnp.float32)
            nangle = pos[:, None] * angle[None, :]
            sin = jnp.sin(nangle)[None, :, None, :]
            cos = jnp.cos(nangle)[None, :, None, :]
            x0 = x[..., 0::2]
            x1 = x[..., 1::2]
            rot = jnp.stack([x0 * cos - x1 * sin, x0 * sin + x1 * cos], axis=-1)
            return rot.reshape(b, s, h, dh)

        def decay_mask(nseq, scale):
            idx = jnp.arange(nseq)
            diff = idx[:, None] - idx[None, :]
            mask = (diff >= 0).astype(scale.dtype)
            diff_c = jnp.maximum(diff, 0).astype(scale.dtype)
            logd = diff_c[None, :, :] * jnp.log(scale)[:, None, None]
            return jnp.exp(logd) * mask[None, :, :]

        def group_norm(R, gamma, beta, nheads):
            b, s, d = R.shape
            dh = d // nheads
            Rg = R.reshape(b, s, nheads, dh)
            mu = jnp.mean(Rg, axis=-1, keepdims=True)
            var = jnp.var(Rg, axis=-1, keepdims=True)
            Rn = (Rg - mu) * jax.lax.rsqrt(var + EPS)
            Rn = Rn * gamma.reshape(1, 1, nheads, dh) + beta.reshape(1, 1, nheads, dh)
            return Rn.reshape(b, s, d)
        key = jax.random.key(seed)
        ks = jax.random.split(key, 7)
        b, s, d, h = (2, 256, 128, 16)
        dh = d // h
        x = jax.random.normal(ks[0], (b, s, d), dtype=jnp.float32)
        std_qkv = float(np.sqrt(2.0 / (dh + d)))
        std_o = float(np.sqrt(2.0 / (d + d)))
        WQ = jax.random.normal(ks[1], (h, dh, d), dtype=jnp.float32) * std_qkv
        WK = jax.random.normal(ks[2], (h, dh, d), dtype=jnp.float32) * std_qkv
        WV = jax.random.normal(ks[3], (h, dh, d), dtype=jnp.float32) * std_qkv
        WO = jax.random.normal(ks[4], (d, d), dtype=jnp.float32) * std_o
        gamma = jnp.ones((d,), dtype=jnp.float32)
        beta = jnp.zeros((d,), dtype=jnp.float32)
        return {'x': x, 'WQ': WQ, 'WK': WK, 'WV': WV, 'WO': WO, 'gamma': gamma, 'beta': beta}
    _L0_attn_in = _L0_attn_setup()

    def _L0_ffn_setup():
        import jax, jax.numpy as jnp
        import numpy as np
        HIDDEN, FFN, N_EXPERTS, TOP_K = (128, 512, 8, 2)
        key = jax.random.key(seed)
        ks = jax.random.split(key, 8)
        s_h = 1.0 / np.sqrt(HIDDEN)
        s_f = 1.0 / np.sqrt(FFN)
        return {'x': jax.random.normal(ks[0], (1, 128, HIDDEN), dtype=jnp.float32), 'gate_w': jax.random.normal(ks[1], (N_EXPERTS, HIDDEN), dtype=jnp.float32) * s_h, 'gate_b': jnp.zeros((N_EXPERTS,), dtype=jnp.float32), 'w1': jax.random.normal(ks[2], (N_EXPERTS, HIDDEN, FFN), dtype=jnp.float32) * s_h, 'b1': jnp.zeros((N_EXPERTS, FFN), dtype=jnp.float32), 'w2': jax.random.normal(ks[3], (N_EXPERTS, FFN, HIDDEN), dtype=jnp.float32) * s_f, 'b2': jnp.zeros((N_EXPERTS, HIDDEN), dtype=jnp.float32)}
    _L0_ffn_in = _L0_ffn_setup()
    _d = {'L0_attn_x': _L0_attn_in['x'], 'L0_attn_WQ': _L0_attn_in['WQ'], 'L0_attn_WK': _L0_attn_in['WK'], 'L0_attn_WV': _L0_attn_in['WV'], 'L0_attn_WO': _L0_attn_in['WO'], 'L0_attn_gamma': _L0_attn_in['gamma'], 'L0_attn_beta': _L0_attn_in['beta'], 'L0_ffn_gate_w': _L0_ffn_in['gate_w'], 'L0_ffn_gate_b': _L0_ffn_in['gate_b'], 'L0_ffn_w1': _L0_ffn_in['w1'], 'L0_ffn_b1': _L0_ffn_in['b1'], 'L0_ffn_w2': _L0_ffn_in['w2'], 'L0_ffn_b2': _L0_ffn_in['b2']}
    _x0 = _d['L0_attn_x']
    _d['L0_attn_x'] = jax.random.normal(jax.random.fold_in(jax.random.key(seed), 1), (8, 1024, 128), dtype=_x0.dtype)
    del _x0
    return _d

def reference(L0_attn_x, L0_attn_WQ, L0_attn_WK, L0_attn_WV, L0_attn_WO, L0_attn_gamma, L0_attn_beta, L0_ffn_gate_w, L0_ffn_gate_b, L0_ffn_w1, L0_ffn_b1, L0_ffn_w2, L0_ffn_b2):

    def _L0_attn_ref(x, WQ, WK, WV, WO, gamma, beta):
        import jax, jax.numpy as jnp
        import numpy as np
        EPS = 1e-05

        def xpos_rotate(x, offset=0, conjugate=False):
            b, s, h, dh = x.shape
            expoent = jnp.arange(0, dh, 2, dtype=jnp.float32) / dh
            angle = 10.0 ** (-4.0 * expoent)
            if conjugate:
                angle = -angle
            pos = jnp.arange(offset, s + offset, dtype=jnp.float32)
            nangle = pos[:, None] * angle[None, :]
            sin = jnp.sin(nangle)[None, :, None, :]
            cos = jnp.cos(nangle)[None, :, None, :]
            x0 = x[..., 0::2]
            x1 = x[..., 1::2]
            rot = jnp.stack([x0 * cos - x1 * sin, x0 * sin + x1 * cos], axis=-1)
            return rot.reshape(b, s, h, dh)

        def decay_mask(nseq, scale):
            idx = jnp.arange(nseq)
            diff = idx[:, None] - idx[None, :]
            mask = (diff >= 0).astype(scale.dtype)
            diff_c = jnp.maximum(diff, 0).astype(scale.dtype)
            logd = diff_c[None, :, :] * jnp.log(scale)[:, None, None]
            return jnp.exp(logd) * mask[None, :, :]

        def group_norm(R, gamma, beta, nheads):
            b, s, d = R.shape
            dh = d // nheads
            Rg = R.reshape(b, s, nheads, dh)
            mu = jnp.mean(Rg, axis=-1, keepdims=True)
            var = jnp.var(Rg, axis=-1, keepdims=True)
            Rn = (Rg - mu) * jax.lax.rsqrt(var + EPS)
            Rn = Rn * gamma.reshape(1, 1, nheads, dh) + beta.reshape(1, 1, nheads, dh)
            return Rn.reshape(b, s, d)
        b, s, d = x.shape
        h, dh, _ = WQ.shape
        Q = jnp.einsum('bsd,hud->bshu', x, WQ)
        K = jnp.einsum('bsd,hud->bshu', x, WK)
        V = jnp.einsum('bsd,hud->bshu', x, WV)
        Q = xpos_rotate(Q)
        K = xpos_rotate(K)
        QK = jnp.einsum('bihd,bjhd->bhij', Q, K)
        scale = 1.0 - 2.0 ** (-5.0 - jnp.arange(h, dtype=jnp.float32))
        D = decay_mask(s, scale)
        QKD = QK * D[None]
        R = jnp.einsum('bhij,bjhd->bihd', QKD, V)
        R = R.reshape(b, s, d)
        R = group_norm(R, gamma, beta, h)
        y = R @ WO
        return y

    def _L0_ffn_ref(x, gate_w, gate_b, w1, b1, w2, b2):
        import jax, jax.numpy as jnp
        import numpy as np
        HIDDEN, FFN, N_EXPERTS, TOP_K = (128, 512, 8, 2)
        B, S, H = x.shape
        x_flat = x.reshape(-1, H)
        logits = x_flat @ gate_w.T + gate_b
        top_w, sel = jax.lax.top_k(logits, TOP_K)
        rw = jax.nn.softmax(top_w, axis=-1)
        combine = jnp.sum(jax.nn.one_hot(sel, N_EXPERTS, dtype=x.dtype) * rw[..., None], axis=1)
        h = jax.nn.gelu(jnp.einsum('th,ehf->tef', x_flat, w1) + b1, approximate=False)
        y = jnp.einsum('tef,efh->teh', h, w2) + b2
        out = jnp.einsum('te,teh->th', combine, y)
        return out.reshape(B, S, H)
    x = L0_attn_x
    xn = _layernorm(x, axis=-1)
    s = _L0_attn_ref(xn, L0_attn_WQ, L0_attn_WK, L0_attn_WV, L0_attn_WO, L0_attn_gamma, L0_attn_beta)
    g = _silu(_L0_ffn_ref(xn, L0_ffn_gate_w, L0_ffn_gate_b, L0_ffn_w1, L0_ffn_b1, L0_ffn_w2, L0_ffn_b2))
    x = x + s * g
    return x

_drawn_inputs = setup_inputs


def setup_inputs(seed=0):
    import zlib

    import numpy as np

    out = dict(_drawn_inputs(seed))
    spreads = {'L0_attn_gamma': (1.0, 0.2),
     'L0_attn_beta': (0.0, 0.375),
     'L0_ffn_gate_b': (0.0, 0.1),
     'L0_ffn_b1': (0.0, 0.285),
     'L0_ffn_b2': (0.0, 0.1)}
    factors = {}
    for name, (base, spread) in spreads.items():
        noise = np.random.default_rng([zlib.crc32(name.encode()), seed]).standard_normal(out[name].shape)
        drawn = base * np.exp(spread * noise) if base else spread * noise
        out[name] = jnp.asarray(drawn.astype(out[name].dtype))
    for name, factor in factors.items():
        out[name] = (out[name] * factor).astype(out[name].dtype)
    return out
```

```python
import numpy as np
import concourse.bass as bass
from concourse import mybir
from contextlib import ExitStack

NSEQ, SEQ, DM = 8, 1024, 128
NH, DH = 16, 8
NE, FF, TOPK = 8, 512, 2
P = 128
TOK = NSEQ * SEQ
NT = TOK // P
FC = FF // P
CH = 64
EPS = 1e-5
ET = 256
ES = ET // P
NET = -(-((TOK * TOPK + NE * (ET - 1)) // ET) // 2) * 2
ROW = DM + 4
W1W, W2W = FF + FC, FF + DM
WROW = W1W + W2W
LG = 4
NPAIR = NT // 2
QPS = SEQ // (2 * P)
BIG = 3.0e38
MAGIC = float(2 ** 23)


def head_of(f):
    gp, par, hh = f // 64, (f // 32) % 2, (f // 8) % 4
    return 8 * gp + 2 * hh + par


def constants():
    f32 = np.float32
    c = {}
    part = np.arange(P)
    gam = 1.0 - 2.0 ** (-5.0 - np.arange(NH, dtype=np.float64))
    feat = np.arange(DM)
    hf = np.array([head_of(f) for f in feat])
    dim = feat % DH
    angle = (10.0 ** (-4.0 * (np.arange(0, DH, 2, dtype=f32) / f32(DH)))).astype(f32)
    pos = np.arange(SEQ, dtype=f32)
    nang = (pos[:, None] * angle[None, :]).astype(f32).astype(np.float64)
    cos, sin = np.cos(nang), np.sin(nang)
    ct = np.zeros((P, QPS, 2, 2, DM)); st = np.zeros_like(ct); kg = np.zeros((P, QPS, 2, NH))
    blk = hf[::DH]
    for q in range(QPS):
        for a in range(2):
            ps = (2 * q + a) * P + part
            rel = (ps % CH) - CH // 2
            for qk, sgn in ((0, 1.0), (1, -1.0)):
                dec = gam[hf][None, :] ** (sgn * rel[:, None])
                ct[:, q, qk, a] = cos[ps][:, dim // 2] * dec
                st[:, q, qk, a] = sin[ps][:, dim // 2] * dec * np.where(dim % 2 == 0, -1.0, 1.0)
            kg[:, q, a] = gam[blk][None, :] ** (-1.0 * CH * (ps // CH)[:, None])
    c["cos"], c["sin"] = ct.reshape(P, -1), st.reshape(P, -1)
    c["kgrow"] = kg.reshape(P, -1)
    c["sdec"] = gam[hf][:, None] ** (1.0 * CH * np.arange(SEQ // CH)[None, :])
    c["smask"] = hf[:, None] == (feat // DH)[None, :]
    c["causal"] = np.arange(CH)[None, :] >= (part % CH)[:, None]
    c["ident"] = np.eye(P)
    c["before"] = part[:, None] < part[None, :]
    c["ones"] = np.ones((P, P))
    c["tlt"] = part[:, None] < np.arange(NT)[None, :]
    c["eps"] = np.full((P, 1), EPS)
    c["rev"] = np.broadcast_to(NE - np.arange(NE), (P, NE))
    c["elt"] = np.broadcast_to((np.arange(NE)[None, :] < np.arange(NE)[:, None]).reshape(1, -1), (P, NE * NE))
    tok = np.arange(NT)[None, :] * P + part[:, None]
    c["dest"] = np.stack([tok - TOPK * TOK, tok + TOK - TOPK * TOK], -1).reshape(P, -1)
    c["gidx"] = np.broadcast_to(np.arange(NET), (P, NET))
    at, off = {}, 0
    for n, a in c.items():
        at[n] = (off, a.shape[1]); off += a.shape[1]
    return np.concatenate([np.asarray(a, f32) for a in c.values()], 1).astype(f32), at


def moe_retention(nc, x, WQ, WK, WV, WO, gamma, beta, gate_w, gate_b, w1, b1, w2, b2, tables, out, AT):
    f32, f16, u32, i32 = mybir.dt.float32, mybir.dt.float16, mybir.dt.uint32, mybir.dt.int32
    ALU, ACT, AX = mybir.AluOpType, mybir.ActivationFunctionType, mybir.AxisListType
    ds = bass.ds
    ctx = ExitStack()
    sb = lambda n, s, d=f32: ctx.enter_context(nc.sbuf_tensor(n, s, d))
    dram = lambda n, s: nc.dram_tensor(n, s, f32, kind="Internal").ap()
    sems = {}

    def sem(n):
        if n not in sems:
            sems[n] = ctx.enter_context(nc.semaphore(n))
        return sems[n]

    def due(v):
        return not isinstance(v, int) or v > 0

    def even(i, off):
        return 2 * i + off // 2

    xn_d = dram("xn_d", (TOK, DM))
    xnT_d = dram("xnT_d", (P, TOK))
    xs_d = dram("xs_d", (NET * ET, ROW))
    y_d = dram("y_d", (TOPK * TOK, DM))
    s_d = dram("s_d", (TOK, DM))

    def by_tile(a):
        return a.rearrange("(t p) d -> p t d", p=P)

    def turns(eng, count, body):
        body(0)
        with eng.Fori(1, count) as i:
            body(i)

    with ctx:
        tab = sb("tab", [P, tables.shape[1]])

        def T(n, p=P):
            o, w = AT[n]
            return tab[0:p, o:o + w]

        ident, ones = T("ident"), T("ones")
        ident16 = sb("ident16", [P, P], f16)
        wrow = sb("wrow", [P, 4, DM])
        wqk = sb("wqk", [P, 2, DM])
        wvc = sb("wvc", [P, DM])
        wvp = sb("wvp", [P, 2, CH])
        gwr = sb("gwr", [NE, DM])
        gwT = sb("gwT", [P, NE])
        gbb = sb("gbb", [P, NE])
        gcol = sb("gcol", [P, 2])
        stage = sb("stage", [P, NE, WROW])
        zero = sb("zero", [P, 1188])
        x4 = sb("x4", [P, 2, LG, DM])
        xn4 = sb("xn4", [P, 2, LG, DM])
        xT4 = sb("xT4", [P, 2, LG * P])
        bst = sb("bst", [P, LG, 6])
        bmv = sb("bmv", [P, LG, 2])
        std4 = sb("std4", [P, LG])
        rstd4 = sb("rstd4", [P, LG])
        logits = sb("logits", [P, NT, NE])
        oh1 = sb("oh1", [P, NT, NE]); oh2 = sb("oh2", [P, NT, NE])
        ra = sb("ra", [P, NT, NE]); rb = sb("rb", [P, NT, NE])
        m1 = sb("m1", [P, NT]); m2 = sb("m2", [P, NT]); mr = sb("mr", [P, NT])
        ew = sb("ew", [P, NT]); den = sb("den", [P, NT])
        cnt = sb("cnt", [NT, NE]); cm = sb("cm", [NT, NT, NE])
        tiles = sb("tiles", [P, NE]); first = sb("first", [P, NE]); last = sb("last", [P, NE])
        tri = sb("tri", [P, NE, NE])
        posf = sb("posf", [P, NT, TOPK])
        posu = sb("posu", [P, NT, TOPK], u32)
        meta = sb("meta", [P, NT, TOPK, ROW - DM])
        tcmp = sb("tcmp", [1, NET, NE]); tmf = sb("tmf", [1, NET]); tmap = sb("tmap", [1, NET], i32)
        wmin = sb("wmin", [P, 1]); wmax = sb("wmax", [P, 1]); wmaxa = sb("wmaxa", [P, 1])
        sq_scale = sb("sq_scale", [P, 1]); unscale = sb("unscale", [P, 1]); vmean = sb("vmean", [P, NH])
        xin = sb("xin", [P, 2, 2 * P])
        t1 = sb("t1", [P, 512]); t2 = sb("t2", [P, 512])
        qf = sb("qf", [P, 2, 2, 2 * DM])
        slots = sb("slots", [P, 2, 2, 2, NH, 4, DH], f16)
        qkT = sb("qkT", [P, 2, 2, 2, 4, P], f16)
        vexp = sb("vexp", [P, 2, 4, DM])
        vpl = sb("vpl", [P, 2, 2, DM])
        kst = sb("kst", [P, 2, 2, NH, DH])
        qT = sb("qT", [P, 2, 2 * P])
        prob = sb("prob", [P, 4, 512])
        sg = sb("sg", [P, 2, DM])
        sqr = sb("sqr", [P, 2 * DM]); ssum = sb("ssum", [P, 32]); rn_std = sb("rn_std", [P, 32])
        rn = sb("rn", [P, 2 * DM]); rnT = sb("rnT", [P, 2 * P])
        sout = sb("sout", [P, 2, 2, DM])
        rows = sb("rows", [P, 2, 2, TOPK, ROW])
        sidx = sb("sidx", [P, 2, 2 * TOPK], u32)
        wb1 = sb("wb1", [P, 2, W1W]); wb2 = sb("wb2", [P, 2, W2W])
        mt = sb("mt", [P, 2, ES, 2])
        xr = sb("xr", [P, 2, ES, ROW])
        xT = sb("xT", [P, 2, ET])
        hT = sb("hT", [P, 2, FC, ET])
        ya = sb("ya", [P, ES, DM])
        yb = sb("yb", [P, 2, ES, DM])
        yi = sb("yi", [P, 2, ES], u32)
        ly = sb("ly", [P, 2, 2, LG, DM]); ls = sb("ls", [P, 2, LG, DM]); lx = sb("lx", [P, 2, LG, DM])
        lu = sb("lu", [P, LG, DM]); lg = sb("lg", [P, LG, DM]); lo = sb("lo", [P, 2, LG, DM])

        BK = [ctx.enter_context(nc.psum_tensor(f"bank{i}", [P, 512], f32)) for i in range(8)]
        BS, BST, BA, BB, BC = BK[0:4], BK[4], BK[5], BK[6], BK[7]

        block = ctx.enter_context(nc.Block())

        @block.sync
        def _(eng):
            eng.dma_start(tab[:], tables).then_inc(sem("tables"), 16)
            for i, w in enumerate((WQ, WK, WV)):
                eng.dma_start(wrow[:, i, :], w.rearrange("h u d -> (h u) d")).then_inc(sem("weights"), 16)
            eng.dma_start(wrow[:, 3, :], WO).then_inc(sem("weights"), 16)
            eng.dma_start(gwr[:], gate_w).then_inc(sem("weights"), 16)
            eng.dma_start(gbb[:], gate_b.rearrange("(o e) -> o e", o=1).broadcast_to([P, NE])).then_inc(sem("weights"), 16)
            eng.dma_start(gcol[:, 0:1], gamma.rearrange("(p o) -> p o", o=1)).then_inc(sem("weights"), 16)
            eng.dma_start(gcol[:, 1:2], beta.rearrange("(p o) -> p o", o=1)).then_inc(sem("weights"), 16)

            def ln_load(n, par):
                eng.dma_start(x4[:, par], by_tile(x)[:, ds(n * LG, LG), :]).then_inc(sem(f"x_in{par}"), 16)

            def ln_store(n, par, more):
                eng.wait_ge(sem("xn"), n + 1)
                eng.dma_start(by_tile(xn_d)[:, ds(n * LG, LG), :], xn4[:, par]).then_inc(sem(f"xn_out{par}"), 16)
                if more:
                    ln_load(n + 2, par)
                eng.wait_ge(sem("xT4"), n + 1)
                eng.dma_start(xnT_d[:, ds(n * LG * P, LG * P)], xT4[:, par]).then_inc(sem(f"xT_out{par}"), 16)

            ln_load(0, 0)
            ln_load(1, 1)
            def body(i):
                for par in range(2):
                    ln_store(2 * i + par, par, True)

            turns(eng, NT // (2 * LG) - 1, body)
            for par in range(2):
                ln_store(NT // LG - 2 + par, par, False)
            for par in range(2):
                eng.wait_ge(sem(f"xn_out{par}"), 16 * NT // (2 * LG))
                eng.wait_ge(sem(f"xT_out{par}"), 16 * NT // (2 * LG))

            def step_loads(i, off):
                m, par = QPS * i + off, off % 2
                if due(m - 1):
                    eng.wait_ge(sem("v"), m - 1)
                eng.dma_start(xin[:, par], xnT_d[:, ds(m * 2 * P, 2 * P)]).then_inc(sem(f"xin{par}"), 16)
                for a in range(4):
                    if due(16 * even(i, off)):
                        eng.wait_ge(sem(f"sent{par}{a}"), 16 * even(i, off))
                for k in range(TOPK):
                    eng.dma_start(rows[:, par, :, k, 0:DM], by_tile(xn_d)[:, ds(2 * m, 2), :]).then_inc(sem(f"rows{par}"), 16)

            def s_store(m, par):
                eng.wait_ge(sem("s_ev"), m + 1)
                eng.dma_start(by_tile(s_d)[:, ds(2 * m, 2), :], sout[:, par]).then_inc(sem(f"s_out{par}"), 16)

            step_loads(0, 0)
            step_loads(0, 1)
            def body(i):
                for q in range(QPS):
                    step_loads(i, q + 2)
                    s_store(QPS * i + q, q % 2)

            turns(eng, NPAIR // QPS - 1, body)
            for n in range(NPAIR - QPS, NPAIR):
                if n + 2 < NPAIR:
                    step_loads(0, n + 2)
                s_store(n, n % 2)
            for par in range(2):
                eng.wait_ge(sem(f"s_out{par}"), 16 * NPAIR // 2)
                for a in range(4):
                    eng.wait_ge(sem(f"sent{par}{a}"), 16 * NPAIR // 2)

            def tile_loads(g, par):
                if due(g - 1):
                    eng.wait_ge(sem("xtp"), g - 1)
                if due(g - 1):
                    eng.wait_ge(sem("mt"), g - 1)
                eng.dma_start(xr[:, par], xs_d[ds(g * ET, ET), :].rearrange("(s p) d -> p s d", p=P)).then_inc(sem(f"xr{par}"), 16)
                e = eng.value_load(tmap[0:1, ds(g, 1)], min_val=0, max_val=NE - 1)
                if due(FC * (g - 1)):
                    eng.wait_ge(sem("h"), FC * (g - 1))
                eng.dma_start(wb1[:, par], stage[:, ds(e, 1), 0:W1W].rearrange("p o w -> p (o w)")).then_inc(sem(f"wb1{par}"), 16)
                if due(g - 1):
                    eng.wait_ge(sem("ya"), g - 1)
                eng.dma_start(wb2[:, par], stage[:, ds(e, 1), W1W:WROW].rearrange("p o w -> p (o w)")).then_inc(sem(f"wb2{par}"), 16)

            eng.wait_ge(sem("tmap"), 1)
            eng.wait_ge(sem("staged"), 16 * (2 + 2 * NE))
            tile_loads(0, 0)
            tile_loads(1, 1)
            def body(i):
                for par in range(2):
                    tile_loads(2 * i + par + 2, par)

            turns(eng, NET // 2 - 1, body)

            for par in range(2):
                for s in range(ES):
                    eng.wait_ge(sem(f"ys{par}{s}"), 16 * NET // 2)

            def last_loads(n, par):
                if due(n - 1):
                    eng.wait_ge(sem("l_used"), n - 1)
                for k in range(TOPK):
                    eng.dma_start(ly[:, par, k], by_tile(y_d)[:, ds(n * LG + k * NT, LG), :]).then_inc(sem(f"l_in{par}"), 16)
                eng.dma_start(ls[:, par], by_tile(s_d)[:, ds(n * LG, LG), :]).then_inc(sem(f"l_in{par}"), 16)
                eng.dma_start(lx[:, par], by_tile(x)[:, ds(n * LG, LG), :]).then_inc(sem(f"l_in{par}"), 16)

            def last_store(n, par):
                eng.wait_ge(sem("l_used"), n + 1)
                eng.dma_start(by_tile(out)[:, ds(n * LG, LG), :], lo[:, par]).then_inc(sem(f"l_out{par}"), 16)

            last_loads(0, 0)
            last_loads(1, 1)
            def body(i):
                for par in range(2):
                    last_store(2 * i + par, par)
                    last_loads(2 * i + par + 2, par)

            turns(eng, NT // (2 * LG) - 1, body)
            for par in range(2):
                last_store(NT // LG - 2 + par, par)
            for par in range(2):
                eng.wait_ge(sem(f"l_out{par}"), 16 * NT // (2 * LG))

        @block.gpsimd
        def _(eng):
            eng.memset(zero[:], 0.0).then_inc(sem("zero"), 1)
            eng.memset(slots[:, 0], 0.0).then_inc(sem("slots0"), 1)
            eng.memset(vexp[:], 0.0).then_inc(sem("slots0"), 1)
            eng.memset(slots[:, 1], 0.0).then_inc(sem("slots0"), 1)
            eng.wait_ge(sem("tables"), 16)
            eng.tensor_copy(ident16[:], ident).then_inc(sem("ident16"), 1)
            eng.wait_ge(sem("wmax"), 1)
            eng.partition_all_reduce(wmaxa[:], wmax[:], P, bass.bass_isa.ReduceOp.max).then_inc(sem("wmaxa"), 1)

            def feed(i, off):
                m, par = QPS * i + off, off % 2
                eng.wait_ge(sem("rot"), m + 1)
                if due(4 * (m - 1)):
                    eng.wait_ge(sem("kv"), 4 * (m - 1))
                eng.tensor_tensor(kst[:, par].rearrange("p a h d -> p (a h) d"),
                                  qf[:, par, 1, :].rearrange("p (n d) -> p n d", d=DH),
                                  T("kgrow").rearrange("p (q n o) -> p q n o", q=QPS, o=1)[:, off % QPS].broadcast_to([P, 2 * NH, DH]),
                                  ALU.mult).then_inc(sem("kst"), 1)
                eng.wait_ge(sem(f"rows{par}"), 32 * (even(i, off) + 1))
                eng.tensor_copy(rows[:, par].rearrange("p a k r -> p (a k) r")[:, :, DM:ROW],
                                meta[:, ds(2 * m, 2)].rearrange("p a k r -> p (a k) r")).then_inc(sem("meta_in"), 1)
                eng.tensor_copy(sidx[:, par], posu[:, ds(2 * m, 2)].rearrange("p a k -> p (a k)")).then_inc(sem("meta_in"), 1)
                eng.wait_ge(sem("meta_in"), 2 * (m + 1))
                eng.sem_inc(sem("meta_in_seen"), 1)
                for a in range(2):
                    for k in range(TOPK):
                        j = TOPK * a + k
                        eng.indirect_dma_start(xs_d, bass.IndirectOffsetOnAxis(ap=sidx[:, par, j:j + 1], axis=0),
                                               rows[:, par, a, k, :], None).then_inc(sem(f"sent{par}{j}"), 16)

            eng.wait_ge(sem("meta"), 1)
            eng.wait_ge(sem("xs_zeroed"), 16)
            feed(0, 0)
            def body(i):
                for q in range(QPS):
                    feed(i, q + 1)

            turns(eng, NPAIR // QPS - 1, body)
            for n in range(NPAIR - QPS, NPAIR - 1):
                feed(0, n + 1)

            def give(g, par):
                eng.wait_ge(sem("yb"), g + 1)
                eng.sem_inc(sem("yb_seen"), 1)
                for s in range(ES):
                    eng.indirect_dma_start(y_d, bass.IndirectOffsetOnAxis(ap=yi[:, par, s:s + 1], axis=0),
                                           yb[:, par, s, :], None, bounds_check=TOPK * TOK - 1,
                                           oob_is_err=False).then_inc(sem(f"ys{par}{s}"), 16)

            def body(i):
                for par in range(2):
                    give(2 * i + par, par)

            turns(eng, NET // 2, body)

        @block.scalar
        def _(eng):
            eng.dma_start(stage[:, :, 0:FF], w1.rearrange("e d f -> d e f")).then_inc(sem("staged"), 16)
            for e in range(NE):
                eng.dma_start(stage[:, e, FF:W1W], b1[e].rearrange("(c p) -> p c", p=P),
                              allow_slow_non_contiguous=True).then_inc(sem("staged"), 16)
                eng.dma_start(stage[:, e, W1W:W1W + FF].rearrange("p (c h) -> p c h", c=FC),
                              w2[e].rearrange("(c p) h -> p c h", p=P)).then_inc(sem("staged"), 16)
            eng.dma_start(stage[:, :, W1W + FF:WROW],
                          b2.rearrange("(o e) h -> o e h", o=1).broadcast_to([P, NE, DM])).then_inc(sem("staged"), 16)
            eng.wait_ge(sem("zero"), 1)
            eng.dma_start(xs_d.rearrange("(p r) d -> p (r d)", p=P).rearrange("p (o w) -> p o w", w=zero.shape[1]),
                          zero[:].rearrange("p (o w) -> p o w", o=1).broadcast_to([P, NET * ET * ROW // P // zero.shape[1], zero.shape[1]])).then_inc(sem("xs_zeroed"), 16)

            def body(i):
                for par in range(2):
                    n = 2 * i + par
                    eng.wait_ge(sem("bn"), (LG + 1) * (n + 1))
                    if due(n):
                        eng.wait_ge(sem("lnr"), n)
                    eng.activation(std4[:], bmv[:, :, 1], ACT.Sqrt, bias=T("eps")).then_inc(sem("ln_std"), 1)
                    eng.wait_ge(sem("ln_tp"), n + 1)
                    if due(16 * i):
                        eng.wait_ge(sem(f"xT_out{par}"), 16 * i)
                    eng.activation(xT4[:, par], BS[par][:], ACT.Copy).then_inc(sem("xT4"), 1)

            turns(eng, NT // (2 * LG), body)
            eng.wait_ge(sem("dm"), 1)
            eng.activation(ew[:], m2[:], ACT.Exp).then_inc(sem("ew"), 1)

            def front_h(m, par):
                eng.wait_ge(sem("rot"), m + 1)
                if due(2 * (m - 1)):
                    eng.wait_ge(sem("tp"), 2 * (m - 1))
                for qk, sl in ((0, slice(0, 2)), (1, slice(0, 3, 2))):
                    src = qf[:, par, qk, :].rearrange("p (n o d) -> p n o d", o=1, d=DH).broadcast_to([P, 2 * NH, 2, DH])
                    dst = slots[:, par, qk].rearrange("p a h s d -> p (a h) s d")[:, :, sl, :]
                    eng.activation(dst, src, ACT.Copy).then_inc(sem("hi"), 1)

            def v_ev(m, par):
                eng.wait_ge(sem("v"), m + 1)
                if due(m - 1):
                    eng.wait_ge(sem("R"), m - 1)
                for pr in range(2):
                    h = slice(CH * pr, CH * pr + CH)
                    eng.activation(vexp[h, par].rearrange("p c (m r d) -> p (c m) r d", r=2, d=DH)[:, :, pr, :],
                                   BB[h, 0:256].rearrange("p (n d) -> p n d", d=DH), ACT.Copy)
                eng.activation(vpl[:, par].rearrange("p a d -> p (a d)"), BB[:, 256:512], ACT.Copy).then_inc(sem("vexp"), 1)

            def tp_ev(m, par, a):
                eng.wait_ge(sem("tp"), 2 * m + a + 1)
                if a == 0:
                    if due(4 * (m - 1)):
                        eng.wait_ge(sem("sc"), 4 * (m - 1))
                bank = (BA, BB)[a]
                eng.activation(qkT[:, par, a].rearrange("p k g t -> p (k g t)"),
                               bank[:].bitcast(f16), ACT.Copy).then_inc(sem("tp_ev"), 1)

            def slot(i, q, front, back):
                n, par = QPS * i + q, (q + 1) % 2
                if front:
                    front_h(n + 1, par)
                    v_ev(n + 1, par)
                if back:
                    eng.wait_ge(sem("R"), n + 1)
                    eng.activation(sqr[:], BC[:, 0:256], ACT.Square, scale=unscale[:, 0:1]).then_inc(sem("sqr"), 1)
                    eng.wait_ge(sem("gn"), n + 1)
                    eng.activation(rn_std[:], ssum[:], ACT.Sqrt, scale=1.0 / DH, bias=T("eps")).then_inc(sem("std"), 1)
                if front:
                    tp_ev(n + 1, par, 0)
                eng.wait_ge(sem("qtrt"), n + 2)
                if front:
                    eng.activation(qT[:, par], BC[:, 0:256], ACT.Copy).then_inc(sem("qT"), 1)
                if back:
                    eng.activation(rnT[:], BC[:, 256:512], ACT.Identity, bias=gcol[:, 1:2], scale=gcol[:, 0:1]).then_inc(sem("rnT"), 1)
                if front:
                    tp_ev(n + 1, par, 1)
                if back:
                    eng.wait_ge(sem("s"), n + 1)
                    if due(16 * even(i, q)):
                        eng.wait_ge(sem(f"s_out{1 - par}"), 16 * even(i, q))
                    eng.activation(sout[:, 1 - par].rearrange("p a d -> p (a d)"), BC[:, 0:256], ACT.Copy).then_inc(sem("s_ev"), 1)

            eng.wait_ge(sem("scales"), 1)
            eng.wait_ge(sem("slots0"), 3)
            slot(-1, 3, True, False)
            def body(i):
                for q in range(QPS):
                    slot(i, q, True, True)

            turns(eng, NPAIR // QPS - 1, body)
            for q in range(QPS):
                slot(NPAIR // QPS - 1, q, q + 1 < QPS, True)

            def turn_in(g, par):
                eng.wait_ge(sem("xtp"), g + 1)
                if due(4 * (g - 1)):
                    eng.wait_ge(sem("l1"), 4 * (g - 1))
                eng.activation(xT[:, par], BST[:, 0:256], ACT.Copy).then_inc(sem("xT"), 1)

            def gelu(g, par):
                if due(g - 1):
                    eng.wait_ge(sem("l2"), g - 1)
                for c in range(FC):
                    eng.wait_ge(sem("l1"), FC * g + c + 1)
                    eng.activation(hT[:, par, c], BS[c][:, par * ET:(par + 1) * ET],
                                   ACT.Gelu, bias=wb1[:, par, FF + c:FF + c + 1]).then_inc(sem("h"), 1)

            turn_in(0, 0)
            gelu(0, 0)
            turn_in(1, 1)
            def body(i):
                for par in range(2):
                    gelu(2 * i + par + 1, 1 - par)
                    turn_in(2 * i + par + 2, par)

            turns(eng, NET // 2 - 1, body)
            gelu(NET - 1, 1)

            def body(i):
                for par in range(2):
                    eng.wait_ge(sem("lu"), 2 * i + par + 1)
                    eng.activation(lg[:], lu[:], ACT.Silu).then_inc(sem("lg"), 1)

            turns(eng, NT // (2 * LG), body)

        @block.vector
        def _(eng):
            seq = [0]

            def step(ins):
                seq[0] += 1
                ins.then_inc(sem("dve_step"), 1)
                eng.wait_ge(sem("dve_step"), seq[0])

            eng.wait_ge(sem("weights"), 128)
            eng.wait_ge(sem("tables"), 16)
            step(eng.tensor_reduce(wmaxa[:], wrow[:, 0:2, :], AX.XY, ALU.max))
            step(eng.tensor_reduce(wmin[:], wrow[:, 0:2, :], AX.XY, ALU.min))
            eng.scalar_tensor_tensor(wmax[:], wmin[:], -1.0, wmaxa[:], ALU.mult, ALU.max).then_inc(sem("wmax"), 1)
            eng.wait_ge(sem("wtp"), 4)
            step(eng.tensor_reduce(vmean[:], BK[6][:, 0:DM].rearrange("p (h u) -> p h u", u=DH), AX.X, ALU.add))
            step(eng.tensor_scalar(vmean[:], vmean[:], 1.0 / DH, None, ALU.mult))
            step(eng.tensor_tensor(wvc[:].rearrange("p (h u) -> p h u", u=DH), BK[6][:, 0:DM].rearrange("p (h u) -> p h u", u=DH),
                                   vmean[:].rearrange("p (h o) -> p h o", o=1).broadcast_to([P, NH, DH]), ALU.subtract))
            eng.wait_ge(sem("wmaxa"), 1)
            step(eng.tensor_scalar(wmaxa[:], wmaxa[:], 1e-30, None, ALU.max))
            step(eng.tensor_scalar(wmaxa[:].bitcast(u32), wmaxa[:].bitcast(u32), 0x7F800000, None, ALU.bitwise_and))
            step(eng.reciprocal(sq_scale[:], wmaxa[:]))
            step(eng.tensor_scalar(sq_scale[:], sq_scale[:], 32.0, None, ALU.mult))
            step(eng.tensor_scalar(wmaxa[:], wmaxa[:], 1.0 / 32.0, None, ALU.mult))
            step(eng.tensor_tensor(unscale[:], wmaxa[:], wmaxa[:], ALU.mult))
            step(eng.tensor_tensor(gcol[:, 0:1], gcol[:, 0:1], unscale[:], ALU.mult))
            for pr in range(2):
                step(eng.tensor_copy(wvp[:, pr].rearrange("p (m d) -> p m d", d=DH), wvc[:].rearrange("p (m r d) -> p m r d", r=2, d=DH)[:, :, pr, :]))
            for qk in range(2):
                for gp in range(2):
                    step(eng.tensor_scalar(
                        wqk[:, qk, 64 * gp:64 * gp + 64].rearrange("p (r h u) -> p r h u", r=2, h=4),
                        BK[4 + qk][:, 64 * gp:64 * gp + 64].rearrange("p (h r u) -> p r h u", h=4, r=2),
                        sq_scale[:, 0:1], None, ALU.mult))
            eng.tensor_copy(gwT[:], BK[7][:, 0:NE]).then_inc(sem("scales"), 1)

            def gate_out(n, par):
                eng.wait_ge(sem("lgt"), n + 1)
                eng.tensor_tensor(logits[:, ds(n * LG, LG), :], BS[2 + par][:, 0:LG * NE].rearrange("p (t e) -> p t e", e=NE),
                                  gbb[:].rearrange("p (o e) -> p o e", o=1).broadcast_to([P, LG, NE]), ALU.add).then_inc(sem("logit"), 1)

            def body(i):
                for par in range(2):
                    n = 2 * i + par
                    eng.wait_ge(sem(f"x_in{par}"), 16 * (i + 1))
                    for t in range(LG):
                        eng.bn_stats(bst[:, t], x4[:, par, t]).then_inc(sem("bn"), 1)
                    eng.wait_ge(sem("bn"), (LG + 1) * n + LG)
                    eng.sem_inc(sem("bn_seen"), 1)
                    for t in range(LG):
                        ins = eng.bn_aggr(bmv[:, t], bst[:, t])
                    ins.then_inc(sem("bn"), 1)
                    eng.wait_ge(sem("ln_std"), n + 1)
                    eng.reciprocal(rstd4[:], std4[:]).then_inc(sem("lnr"), 1)
                    eng.wait_ge(sem("lnr"), n + 1)
                    if due(16 * i):
                        eng.wait_ge(sem(f"xn_out{par}"), 16 * i)
                    for t in range(LG):
                        ins = eng.tensor_scalar(xn4[:, par, t], x4[:, par, t], bmv[:, t, 0:1], rstd4[:, t:t + 1], ALU.subtract, ALU.mult)
                    ins.then_inc(sem("xn"), 1)
                    gate_out(n, par)

            turns(eng, NT // (2 * LG), body)

            eng.wait_ge(sem("logit"), NT // LG)
            bc = lambda a: a.rearrange("p (t o) -> p t o", o=1).broadcast_to([P, NT, NE])
            rev = T("rev").rearrange("p (o e) -> p o e", o=1).broadcast_to([P, NT, NE])
            step(eng.tensor_reduce(m1[:], logits[:], AX.X, ALU.max))
            step(eng.tensor_tensor(ra[:], logits[:], bc(m1[:]), ALU.is_equal))
            step(eng.tensor_tensor(rb[:], ra[:], rev, ALU.mult))
            step(eng.tensor_reduce(mr[:], rb[:], AX.X, ALU.max))
            step(eng.tensor_tensor(oh1[:], rev, bc(mr[:]), ALU.is_equal))
            step(eng.scalar_tensor_tensor(ra[:], oh1[:], -BIG, logits[:], ALU.mult, ALU.add))
            step(eng.tensor_reduce(m2[:], ra[:], AX.X, ALU.max))
            step(eng.tensor_tensor(rb[:], ra[:], bc(m2[:]), ALU.is_equal))
            step(eng.tensor_tensor(ra[:], rb[:], rev, ALU.mult))
            step(eng.tensor_reduce(mr[:], ra[:], AX.X, ALU.max))
            step(eng.tensor_tensor(oh2[:], rev, bc(mr[:]), ALU.is_equal))
            step(eng.tensor_tensor(ra[:], oh1[:], oh2[:], ALU.add))
            eng.tensor_tensor(m2[:], m2[:], m1[:], ALU.subtract).then_inc(sem("dm"), 1)
            eng.wait_ge(sem("dm"), 1)
            eng.wait_ge(sem("cnt"), 1)
            step(eng.tensor_copy(cnt[:], BK[4][0:NT, 0:NE]))
            eng.tensor_tensor(cm[:], cnt[:].rearrange("p (o e) -> p o e", o=1).broadcast_to([NT, NT, NE]),
                                   T("tlt", NT).rearrange("p (t o) -> p t o", o=1).broadcast_to([NT, NT, NE]), ALU.mult).then_inc(sem("cm"), 1)
            eng.wait_ge(sem("rank"), 2)
            step(eng.tensor_scalar(tiles[:], BK[6][:, 0:NE], 1.0 / ET, (ET - 1.0) / ET - 0.5 + 0.5 / ET, ALU.mult, ALU.add))
            step(eng.tensor_scalar(tiles[:], tiles[:], MAGIC, None, ALU.add))
            step(eng.tensor_scalar(tiles[:], tiles[:], MAGIC, None, ALU.subtract))
            step(eng.tensor_tensor(tri[:], T("elt").rearrange("p (a b) -> p a b", b=NE),
                                   tiles[:].rearrange("p (o e) -> p o e", o=1).broadcast_to([P, NE, NE]), ALU.mult))
            step(eng.tensor_reduce(first[:], tri[:], AX.X, ALU.add))
            step(eng.tensor_tensor(last[:], first[:], tiles[:], ALU.add))
            step(eng.tensor_scalar(first[:], first[:], float(ET), None, ALU.mult))
            step(eng.tensor_tensor(rb[:], BK[5][:].rearrange("p (t e) -> p t e", e=NE),
                                   first[:].rearrange("p (o e) -> p o e", o=1).broadcast_to([P, NT, NE]), ALU.add))
            for k, oh in enumerate((oh1, oh2)):
                step(eng.tensor_tensor(ra[:], rb[:], oh[:], ALU.mult))
                step(eng.tensor_reduce(posf[:, :, k], ra[:], AX.X, ALU.add))
            step(eng.tensor_copy(posu[:], posf[:]))
            eng.wait_ge(sem("ew"), 1)
            step(eng.tensor_scalar(den[:], ew[:], 1.0, None, ALU.add))
            step(eng.memset(meta[:], 0.0))
            step(eng.reciprocal(meta[:, :, 0, 1], den[:]))
            step(eng.tensor_tensor(meta[:, :, 1, 1], ew[:], meta[:, :, 0, 1], ALU.mult))
            eng.tensor_copy(meta[:, :, :, 0], T("dest").rearrange("p (t k) -> p t k", k=TOPK)).then_inc(sem("meta"), 1)
            step(eng.tensor_tensor(tcmp[:], last[0:1, :].rearrange("p (o e) -> p o e", o=1).broadcast_to([1, NET, NE]),
                                   T("gidx", 1).rearrange("p (t o) -> p t o", o=1).broadcast_to([1, NET, NE]), ALU.is_le))
            step(eng.tensor_reduce(tmf[:], tcmp[:], AX.X, ALU.add))
            eng.tensor_scalar(tmap[:], tmf[:], float(NE - 1), None, ALU.min).then_inc(sem("tmap"), 1)

            causal = T("causal").rearrange("p (o t) -> p o t", o=1).broadcast_to([P, 8, CH])
            smask, sdec = T("smask"), T("sdec")
            cosT = T("cos").rearrange("p (q w) -> p q w", q=QPS)
            sinT = T("sin").rearrange("p (q n two) -> p q n two", q=QPS, two=2)

            def state(n, q, c):
                if due(4 * n + c):
                    eng.wait_ge(sem("kv"), 4 * n + c)
                if q == 0 and c == 0:
                    ins = eng.memset(sg[:, 0], 0.0)
                else:
                    k = 4 * q + c
                    ins = eng.scalar_tensor_tensor(sg[:, c % 2], BST[:, 0:DM], sdec[:, k:k + 1], smask, ALU.mult, ALU.mult)
                ins.then_inc(sem("sg"), 1)

            def slot(i, q, front, back):
                n, m, par, mq = QPS * i + q, QPS * i + q + 1, (q + 1) % 2, (q + 1) % QPS
                if back:
                    state(n, q, 0)
                    for hh in range(4):
                        eng.wait_ge(sem("sc"), 4 * n + hh + 1)
                        if due(n):
                            eng.wait_ge(sem("R"), n)
                        eng.tensor_tensor(prob[:, hh].rearrange("p (b t) -> p b t", t=CH), BS[hh][:].rearrange("p (b t) -> p b t", t=CH),
                                          causal, ALU.mult).then_inc(sem("prob"), 1)
                if front:
                    eng.wait_ge(sem("qk"), m + 1)
                    if due(m):
                        eng.wait_ge(sem("rot"), m)
                    eng.tensor_tensor(t1[:], BA[:], cosT[:, mq], ALU.mult).then_inc(sem("rot_part"), 1)
                if back:
                    state(n, q, 1)
                if front:
                    src = BA[:].rearrange("p (n two) -> p n two", two=2)
                    dst = t2[:].rearrange("p (n two) -> p n two", two=2)
                    for z in range(2):
                        eng.tensor_tensor(dst[:, :, z], src[:, :, 1 - z], sinT[:, mq, :, z], ALU.mult).then_inc(sem("rot_part"), 1)
                if back:
                    state(n, q, 2)
                if front:
                    eng.wait_ge(sem("rot_part"), 3 * (m + 1))
                    if due(m - 1):
                        eng.wait_ge(sem("qtrt"), m - 1)
                    if due(2 * (m - 1)):
                        eng.wait_ge(sem("hi"), 2 * (m - 1))
                    if due(m - 1):
                        eng.wait_ge(sem("kst"), m - 1)
                    eng.tensor_tensor(qf[:, par].rearrange("p k w -> p (k w)"), t1[:], t2[:], ALU.add).then_inc(sem("rot"), 1)
                if back:
                    state(n, q, 3)
                if front:
                    eng.wait_ge(sem("hi"), 2 * (m + 1))
                    for qk, sl in ((0, 2), (1, 1)):
                        s5 = slots[:, par, qk].rearrange("p a h s d -> p (a h) s d")
                        eng.wait_ge(sem("rot"), m + 1)
                        eng.tensor_tensor(s5[:, :, sl, :], qf[:, par, qk, :].rearrange("p (n d) -> p n d", d=DH), s5[:, :, 0, :],
                                          ALU.subtract).then_inc(sem("lo"), 1)
                if back:
                    eng.wait_ge(sem("sqr"), n + 1)
                    eng.tensor_reduce(ssum[:], sqr[:].rearrange("p (n d) -> p n d", d=DH), AX.X, ALU.add).then_inc(sem("gn"), 1)
                    eng.wait_ge(sem("std"), n + 1)
                    eng.reciprocal(ssum[:], rn_std[:]).then_inc(sem("rstd"), 1)
                    eng.wait_ge(sem("rstd"), n + 1)
                    eng.wait_ge(sem("qtrt"), n + 1)
                    eng.tensor_tensor(rn[:].rearrange("p (n d) -> p n d", d=DH), BC[:, 0:256].rearrange("p (n d) -> p n d", d=DH),
                                      ssum[:].rearrange("p (n o) -> p n o", o=1).broadcast_to([P, 32, DH]), ALU.mult).then_inc(sem("rn"), 1)

            slot(-1, 3, True, False)
            def body(i):
                for q in range(QPS):
                    slot(i, q, True, True)

            turns(eng, NPAIR // QPS - 1, body)
            for q in range(QPS):
                slot(NPAIR // QPS - 1, q, q + 1 < QPS, True)

            def take_meta(g, i, par):
                eng.wait_ge(sem(f"xr{par}"), 16 * (i + 1))
                if due(g - 1):
                    eng.wait_ge(sem("yb"), g - 1)
                eng.tensor_copy(mt[:, par], xr[:, par, :, DM:DM + 2]).then_inc(sem("mt"), 1)

            def finish(i, par):
                g = 2 * i + par
                eng.wait_ge(sem("l2"), g + 1)
                eng.wait_ge(sem(f"wb2{par}"), 16 * (i + 1))
                if due(g):
                    eng.wait_ge(sem("yb"), g)
                eng.tensor_tensor(ya[:], (BA, BB)[par][:, 0:ET].rearrange("p (s d) -> p s d", d=DM),
                                  wb2[:, par, FF:W2W].rearrange("p (o d) -> p o d", o=1).broadcast_to([P, ES, DM]),
                                  ALU.add).then_inc(sem("ya"), 1)
                for s in range(ES):
                    if due(16 * i):
                        eng.wait_ge(sem(f"ys{par}{s}"), 16 * i)
                eng.wait_ge(sem("mt"), g + 1)
                eng.tensor_scalar(yi[:, par], mt[:, par, :, 0], float(TOPK * TOK), None, ALU.add).then_inc(sem("yi"), 1)
                eng.wait_ge(sem("ya"), g + 1)
                eng.wait_ge(sem("yi"), g + 1)
                eng.tensor_tensor(yb[:, par], ya[:], mt[:, par, :, 1:2].broadcast_to([P, ES, DM]), ALU.mult).then_inc(sem("yb"), 1)

            take_meta(0, 0, 0)
            take_meta(1, 0, 1)
            def body(i):
                for par in range(2):
                    finish(i, par)
                    take_meta(2 * i + par + 2, i + 1, par)

            turns(eng, NET // 2 - 1, body)
            for par in range(2):
                finish(NET // 2 - 1, par)

            def body(i):
                for par in range(2):
                    n = 2 * i + par
                    eng.wait_ge(sem(f"l_in{par}"), 64 * (i + 1))
                    if due(n):
                        eng.wait_ge(sem("lg"), n)
                    eng.tensor_tensor(lu[:], ly[:, par, 0], ly[:, par, 1], ALU.add).then_inc(sem("lu"), 1)
                    eng.wait_ge(sem("lg"), n + 1)
                    if due(16 * i):
                        eng.wait_ge(sem(f"l_out{par}"), 16 * i)
                    if due(n):
                        eng.wait_ge(sem("l_used"), n)
                    eng.tensor_tensor(ls[:, par], lg[:], ls[:, par], ALU.mult).then_inc(sem("lm"), 1)
                    eng.wait_ge(sem("lm"), n + 1)
                    eng.tensor_tensor(lo[:, par], lx[:, par], ls[:, par], ALU.add).then_inc(sem("l_used"), 1)

            turns(eng, NT // (2 * LG), body)

        @block.tensor
        def _(eng):
            mm = eng.matmul
            eng.wait_ge(sem("tables"), 16)
            eng.wait_ge(sem("weights"), 128)
            for j in range(3):
                eng.transpose(BK[4 + j][:, 0:DM], wrow[:, j, :], ident).then_inc(sem("wtp"), 1)
            eng.transpose(BK[7][:, 0:NE], gwr[:], ident[0:NE, 0:NE]).then_inc(sem("wtp"), 1)

            def logit(n, par):
                eng.wait_ge(sem("xT4"), n + 1)
                if due(n - 1):
                    eng.wait_ge(sem("logit"), n - 1)
                for t in range(LG):
                    ins = mm(BS[2 + par][:, t * NE:(t + 1) * NE], xT4[:, par, t * P:(t + 1) * P], gwT[:], start=True, stop=True)
                ins.then_inc(sem("lgt"), 1)

            eng.wait_ge(sem("scales"), 1)

            def ln_step(n, par):
                eng.wait_ge(sem("xn"), n + 1)
                if due(n - 1):
                    eng.wait_ge(sem("xT4"), n - 1)
                for t in range(LG):
                    ins = eng.transpose(BS[par][:, t * P:(t + 1) * P], xn4[:, par, t], ident)
                ins.then_inc(sem("ln_tp"), 1)
                logit(n, par)

            ln_step(0, 0)
            ln_step(1, 1)
            with eng.Fori(1, NT // (2 * LG)) as i:
                for par in range(2):
                    ln_step(2 * i + par, par)

            eng.wait_ge(sem("dm"), 1)
            for e in range(NE):
                ins = mm(BK[4][0:NT, e:e + 1], ra[:, :, e], ones[:, 0:1], start=True, stop=True)
            ins.then_inc(sem("cnt"), 1)
            mm(BK[5][:], T("before"), ra[:].rearrange("p t e -> p (t e)"), start=True, stop=False)
            eng.wait_ge(sem("cm"), 1)
            mm(BK[5][:], ones[0:NT, :], cm[:].rearrange("p t e -> p (t e)"), start=False, stop=True).then_inc(sem("rank"), 1)
            mm(BK[6][:, 0:NE], ones[0:NT, :], cnt[:], start=True, stop=True).then_inc(sem("rank"), 1)
            eng.wait_ge(sem("meta"), 1)

            def slot(i, q, front, back):
                n, m, par, bp = QPS * i + q, QPS * i + q + 1, (q + 1) % 2, q % 2
                if back:
                    eng.wait_ge(sem("tp_ev"), 2 * (n + 1))
                    for hh in range(4):
                        r = slice(32 * hh, 32 * hh + 32)
                        for c in range(4):
                            a, tk = c // 2, slice(CH * (c % 2), CH * (c % 2) + CH)
                            for g in range(4):
                                pr, gp = g % 2, g // 2
                                o = (c * 2 + gp) * CH
                                ins = mm(BS[hh][CH * pr:CH * pr + CH, o:o + CH], qkT[r, bp, a, 1, g, tk], qkT[r, bp, a, 0, g, tk],
                                         start=True, stop=True)
                        ins.then_inc(sem("sc"), 1)
                if front:
                    eng.wait_ge(sem(f"xin{par}"), 16 * (even(i, q + 1) + 1))
                    if due(2 * m):
                        eng.wait_ge(sem("tp_ev"), 2 * m)
                    for a in range(2):
                        ins = mm(BA[:].rearrange("p (k a d) -> p k a d", k=2, a=2)[:, :, a, :], xin[:, par, a * P:(a + 1) * P],
                                 wqk[:].rearrange("p k d -> p (k d)"), start=True, stop=True)
                    ins.then_inc(sem("qk"), 1)
                    for c in range(4):
                        for pr in range(2):
                            mm(BB[CH * pr:CH * pr + CH, c * CH:(c + 1) * CH], xin[:, par, c * CH:(c + 1) * CH], wvp[:, pr, :],
                               start=True, stop=True)
                    for a in range(2):
                        ins = mm(BB[:, 256 + a * DM:256 + (a + 1) * DM], xin[:, par, a * P:(a + 1) * P], wvc[:], start=True, stop=True)
                    ins.then_inc(sem("v"), 1)
                if back:
                    if due(n):
                        eng.wait_ge(sem("s_ev"), n)
                    eng.wait_ge(sem("kst"), n + 1)
                    eng.wait_ge(sem("qT"), n + 1)
                    eng.wait_ge(sem("vexp"), n + 1)
                    for c in range(4):
                        a, h0 = c // 2, CH * (c % 2)
                        tk = slice(h0, h0 + CH)
                        rows_ = BC[tk, a * DM:(a + 1) * DM]
                        eng.wait_ge(sem("sg"), 4 * n + c + 1)
                        mm(rows_, qT[:, bp, c * CH:(c + 1) * CH], sg[:, c % 2], start=True, stop=False, skip_group_check=True).then_inc(sem("inter"), 1)
                        mm(BST[:, 0:DM], kst[tk, bp, a].rearrange("p h d -> p (h d)"), vpl[tk, bp, a],
                           start=(q == 0 and c == 0), stop=True, skip_group_check=True).then_inc(sem("kv"), 1)
                        eng.wait_ge(sem("prob"), 4 * (n + 1))
                        for pair in range(NH // 2):
                            gp, hh = pair // 4, pair % 4
                            o = (c * 2 + gp) * CH
                            v0 = 2 * DH * pair
                            ins = mm(BC[tk, a * DM + v0:a * DM + v0 + 2 * DH], prob[:, hh, o:o + CH], vexp[:, bp, c, v0:v0 + 2 * DH],
                                     start=False, stop=(pair == NH // 2 - 1), skip_group_check=True)
                    ins.then_inc(sem("R"), 1)

                def turn(a):
                    bank = (BA, BB)[a][:].bitcast(f16)
                    eng.wait_ge(sem("lo"), 2 * (m + 1))
                    eng.wait_ge(sem("hi"), 2 * (m + 1))
                    if a == 0:
                        eng.wait_ge(sem("rot_part"), 3 * (m + 1))
                    else:
                        eng.wait_ge(sem("vexp"), m + 1)
                    for k in range(2):
                        for g in range(4):
                            j = 4 * k + g
                            ins = eng.transpose(bank[:, j * P:(j + 1) * P],
                                                slots[:, par, k, a].rearrange("p h s d -> p (h s d)")[:, g * P:(g + 1) * P], ident16[:])
                    ins.then_inc(sem("tp"), 1)

                if front:
                    turn(0)
                if back:
                    eng.wait_ge(sem("rn"), n + 1)
                if front:
                    for a in range(2):
                        ins = eng.transpose(BC[:, a * P:(a + 1) * P], qf[:, par, 0, a * DM:(a + 1) * DM], ident)
                if back:
                    for a in range(2):
                        ins = eng.transpose(BC[:, 256 + a * P:256 + (a + 1) * P], rn[:, a * DM:(a + 1) * DM], ident)
                ins.then_inc(sem("qtrt"), 1)
                if front:
                    turn(1)
                if back:
                    eng.wait_ge(sem("rnT"), n + 1)
                    if front:
                        eng.wait_ge(sem("qT"), m + 1)
                    for a in range(2):
                        ins = mm(BC[:, a * DM:(a + 1) * DM], rnT[:, a * P:(a + 1) * P], wrow[:, 3, :], start=True, stop=True)
                    ins.then_inc(sem("s"), 1)

            slot(-1, 3, True, False)
            def body(i):
                for q in range(QPS):
                    slot(i, q, True, True)

            turns(eng, NPAIR // QPS - 1, body)
            for q in range(QPS):
                slot(NPAIR // QPS - 1, q, q + 1 < QPS, True)
            eng.wait_ge(sem("s_ev"), NPAIR)
            eng.wait_ge(sem("tp_ev"), 2 * NPAIR)

            def turn_rows(i, off):
                g, par = 2 * i + off, off % 2
                eng.wait_ge(sem(f"xr{par}"), 16 * (i + off // 2 + 1))
                if due(g):
                    eng.wait_ge(sem("xT"), g)
                for s in range(ES):
                    ins = eng.transpose(BST[:, s * P:(s + 1) * P], xr[:, par, s, 0:DM], ident)
                ins.then_inc(sem("xtp"), 1)

            def layer1(i, off):
                g, par = 2 * i + off, off % 2
                eng.wait_ge(sem("xT"), g + 1)
                eng.wait_ge(sem(f"wb1{par}"), 16 * (i + off // 2 + 1))
                for c in range(FC):
                    if due(FC * (g - 1) + c + 1):
                        eng.wait_ge(sem("h"), FC * (g - 1) + c + 1)
                    mm(BS[c][:, par * ET:(par + 1) * ET], wb1[:, par, c * P:(c + 1) * P], xT[:, par], start=True, stop=True).then_inc(sem("l1"), 1)

            def layer2(i, par):
                g, bank = 2 * i + par, (BA, BB)[par]
                eng.wait_ge(sem(f"wb2{par}"), 16 * (i + 1))
                if due(g):
                    eng.wait_ge(sem("ya"), g)
                eng.wait_ge(sem("h"), FC * (g + 1))
                for s in range(ES):
                    for c in range(FC):
                        ins = mm(bank[:, s * DM:(s + 1) * DM], hT[:, par, c, s * P:(s + 1) * P],
                                 wb2[:, par, c * DM:(c + 1) * DM], start=(c == 0), stop=(c == FC - 1))
                ins.then_inc(sem("l2"), 1)

            turn_rows(0, 0)
            layer1(0, 0)
            turn_rows(0, 1)
            def body(i):
                for par in range(2):
                    layer1(i, par + 1)
                    turn_rows(i, par + 2)
                    layer2(i, par)

            turns(eng, NET // 2 - 1, body)
            layer1(NET // 2 - 1, 1)
            layer2(NET // 2 - 1, 0)
            layer2(NET // 2 - 1, 1)


NAMES = ("x", "WQ", "WK", "WV", "WO", "gamma", "beta")
FFN_NAMES = ("gate_w", "gate_b", "w1", "b1", "w2", "b2")


def kernel(**inputs):
    from concourse import bacc
    from concourse.bass_utils import run_bass_kernel_spmd

    nc = bacc.Bacc("TRN2", target_bir_lowering=False, num_devices=1)
    arrays = {f"in_{n}": np.ascontiguousarray(inputs[f"L0_attn_{n}"]) for n in NAMES}
    arrays.update({f"in_{n}": np.ascontiguousarray(inputs[f"L0_ffn_{n}"]) for n in FFN_NAMES})
    arrays["in_x"] = arrays["in_x"].reshape(TOK, DM)
    arrays["tables"], at = constants()
    args = [nc.dram_tensor(n, a.shape, mybir.dt.from_np(a.dtype), kind="ExternalInput").ap() for n, a in arrays.items()]
    out = nc.dram_tensor("out", (TOK, DM), mybir.dt.float32, kind="ExternalOutput").ap()
    moe_retention(nc, *args, out, at)
    r = run_bass_kernel_spmd(nc, [arrays], core_ids=[0])
    return np.asarray(r.results[0]["out"]).reshape(NSEQ, SEQ, DM)
```

```python
import numpy as np
import concourse.bass as bass
from concourse import mybir
from contextlib import ExitStack

NSEQ, SEQ, DM = 8, 1024, 128
NH, DH = 16, 8
NE, FF, TOPK = 8, 512, 2
P = 128
TOK = NSEQ * SEQ
NT = TOK // P
FC = FF // P
CH = 64
EPS = 1e-5
ET = 256
ES = ET // P
EB = 4
NET = -(-((TOK * TOPK + NE * (ET - 1)) // ET) // EB) * EB
ROW = DM + 4
W1W, W2W = FF + FC, FF + DM
WROW = W1W + W2W
LG = 4
LB = 4
NLN = NT // LG
NZ = NE + NET - TOK * TOPK // ET
NPAIR = NT // 2
QPS = SEQ // (2 * P)
BIG = 3.0e38
MAGIC = float(2 ** 23)


def head_of(f):
    gp, par, hh = f // 64, (f // 32) % 2, (f // 8) % 4
    return 8 * gp + 2 * hh + par


def constants():
    f32 = np.float32
    c = {}
    part = np.arange(P)
    gam = 1.0 - 2.0 ** (-5.0 - np.arange(NH, dtype=np.float64))
    feat = np.arange(DM)
    hf = np.array([head_of(f) for f in feat])
    dim = feat % DH
    angle = (10.0 ** (-4.0 * (np.arange(0, DH, 2, dtype=f32) / f32(DH)))).astype(f32)
    pos = np.arange(SEQ, dtype=f32)
    nang = (pos[:, None] * angle[None, :]).astype(f32).astype(np.float64)
    cos, sin = np.cos(nang), np.sin(nang)
    ct = np.zeros((P, QPS, 2, 2, DM)); st = np.zeros_like(ct); kg = np.zeros((P, QPS, 2, NH))
    blk = hf[::DH]
    for q in range(QPS):
        for a in range(2):
            ps = (2 * q + a) * P + part
            rel = (ps % CH) - CH // 2
            for qk, sgn in ((0, 1.0), (1, -1.0)):
                dec = gam[hf][None, :] ** (sgn * rel[:, None])
                ct[:, q, qk, a] = cos[ps][:, dim // 2] * dec
                st[:, q, qk, a] = sin[ps][:, dim // 2] * dec * np.where(dim % 2 == 0, -1.0, 1.0)
            kg[:, q, a] = gam[blk][None, :] ** (-1.0 * CH * (ps // CH)[:, None])
    c["cos"], c["sin"] = ct.reshape(P, -1), st.reshape(P, -1)
    c["kgrow"] = kg.reshape(P, -1)
    c["sdec"] = gam[hf][:, None] ** (1.0 * CH * np.arange(SEQ // CH)[None, :])
    c["smask"] = hf[:, None] == (feat // DH)[None, :]
    c["causal"] = np.arange(CH)[None, :] >= (part % CH)[:, None]
    c["ident"] = np.eye(P)
    c["before"] = part[:, None] < part[None, :]
    c["ones"] = np.ones((P, P))
    c["tlt"] = part[:, None] < np.arange(NT)[None, :]
    c["eps"] = np.full((P, 1), EPS)
    c["rev"] = np.broadcast_to(NE - np.arange(NE), (P, NE))
    c["elt"] = np.broadcast_to((np.arange(NE)[None, :] < np.arange(NE)[:, None]).reshape(1, -1), (P, NE * NE))
    tok = np.arange(NT)[None, :] * P + part[:, None]
    c["dest"] = np.stack([tok - TOPK * TOK, tok + TOK - TOPK * TOK], -1).reshape(P, -1)
    c["gidx"] = np.broadcast_to(np.arange(NET), (P, NET))
    c["dump"] = np.broadcast_to(NET + np.arange(NZ), (P, NZ))
    late = ("cos", "sin", "kgrow", "sdec", "smask", "causal")
    c = {n: c[n] for n in sorted(c, key=lambda n: n in late)}
    at, off = {}, 0
    for n, a in c.items():
        at[n] = (off, a.shape[1]); off += a.shape[1]
    return np.concatenate([np.asarray(a, f32) for a in c.values()], 1).astype(f32), at


def moe_retention(nc, x, WQ, WK, WV, WO, gamma, beta, gate_w, gate_b, w1, b1, w2, b2, tables, out, AT):
    f32, f16, u32, i32 = mybir.dt.float32, mybir.dt.float16, mybir.dt.uint32, mybir.dt.int32
    ALU, ACT, AX = mybir.AluOpType, mybir.ActivationFunctionType, mybir.AxisListType
    ds = bass.ds
    ctx = ExitStack()
    sb = lambda n, s, d=f32: ctx.enter_context(nc.sbuf_tensor(n, s, d))
    dram = lambda n, s: nc.dram_tensor(n, s, f32, kind="Internal").ap()
    sems = {}

    def sem(n):
        if n not in sems:
            sems[n] = ctx.enter_context(nc.semaphore(n))
        return sems[n]

    def due(v):
        return not isinstance(v, int) or v > 0

    def even(i, off):
        return 2 * i + off // 2

    xn_d = dram("xn_d", (TOK, DM))
    xnT_d = dram("xnT_d", (P, TOK))
    xs_d = dram("xs_d", ((NET + NZ) * ET, ROW))
    y_d = dram("y_d", (TOPK * TOK, DM))
    s_d = dram("s_d", (TOK, DM))

    def by_tile(a):
        return a.rearrange("(t p) d -> p t d", p=P)

    def turns(eng, count, body):
        body(0)
        with eng.Fori(1, count) as i:
            body(i)

    with ctx:
        tab = sb("tab", [P, tables.shape[1]])

        def T(n, p=P):
            o, w = AT[n]
            return tab[0:p, o:o + w]

        FIRST = AT["cos"][0]
        ident, ones = T("ident"), T("ones")
        ident16 = sb("ident16", [P, P], f16)
        wrow = sb("wrow", [P, 4, DM])
        wqk = sb("wqk", [P, 2, DM])
        wvc = sb("wvc", [P, DM])
        wvp = sb("wvp", [P, 2, CH])
        gwr = sb("gwr", [NE, DM])
        gwT = sb("gwT", [P, NE])
        gbb = sb("gbb", [P, NE])
        gcol = sb("gcol", [P, 2])
        stage = sb("stage", [P, NE, WROW])
        zero = sb("zero", [P, ES, ROW])
        x4 = sb("x4", [P, LB, LG, DM])
        xn4 = sb("xn4", [P, LB, LG, DM])
        xT4 = sb("xT4", [P, LB, LG * P])
        bst = sb("bst", [P, 2, LG, 6])
        bmv = sb("bmv", [P, 2, LG, 2])
        std4 = sb("std4", [P, 2, LG])
        rstd4 = sb("rstd4", [P, 2, LG])
        logits = sb("logits", [P, NT, NE])
        oh1 = sb("oh1", [P, NT, NE]); oh2 = sb("oh2", [P, NT, NE])
        ra = sb("ra", [P, NT, NE]); rb = sb("rb", [P, NT, NE])
        m1 = sb("m1", [P, NT]); m2 = sb("m2", [P, NT]); mr = sb("mr", [P, NT])
        ew = sb("ew", [P, NT]); den = sb("den", [P, NT])
        cnt = sb("cnt", [NT, NE]); cm = sb("cm", [NT, NT, NE])
        tiles = sb("tiles", [P, NE]); first = sb("first", [P, NE]); last = sb("last", [P, NE])
        tri = sb("tri", [P, NE, NE])
        posf = sb("posf", [P, NT, TOPK])
        posu = sb("posu", [P, NT, TOPK], u32)
        meta = sb("meta", [P, NT, TOPK, ROW - DM])
        tcmp = sb("tcmp", [1, NET, NE]); tmf = sb("tmf", [1, NET]); tmap = sb("tmap", [1, NET], i32)
        zcand = sb("zcand", [1, NZ]); zok = sb("zok", [1, NZ]); zt = sb("zt", [1, NZ], i32)
        wmin = sb("wmin", [P, 1]); wmax = sb("wmax", [P, 1]); wmaxa = sb("wmaxa", [P, 1])
        sq_scale = sb("sq_scale", [P, 1]); unscale = sb("unscale", [P, 1]); vmean = sb("vmean", [P, NH])
        xin = sb("xin", [P, 2, 2 * P])
        t1 = sb("t1", [P, 512]); t2 = sb("t2", [P, 512])
        qf = sb("qf", [P, 2, 2, 2 * DM])
        slots = sb("slots", [P, 2, 2, 2, NH, 4, DH], f16)
        qkT = sb("qkT", [P, 2, 2, 2, 4, P], f16)
        vexp = sb("vexp", [P, 2, 4, DM])
        vpl = sb("vpl", [P, 2, 2, DM])
        kst = sb("kst", [P, 2, 2, NH, DH])
        qT = sb("qT", [P, 2, 2 * P])
        prob = sb("prob", [P, 4, 512])
        sg = sb("sg", [P, 2, DM])
        sqr = sb("sqr", [P, 2 * DM]); ssum = sb("ssum", [P, 32]); rn_std = sb("rn_std", [P, 32])
        rn = sb("rn", [P, 2 * DM]); rnT = sb("rnT", [P, 2 * P])
        sout = sb("sout", [P, 2, 2, DM])
        rows = sb("rows", [P, 2, 2, TOPK, ROW])
        sidx = sb("sidx", [P, 2, 2 * TOPK], u32)
        wb = sb("wb", [P, EB, WROW])
        mt = sb("mt", [P, EB, ES, 2])
        xr = sb("xr", [P, EB, ES, ROW])
        xT = sb("xT", [P, 2, ET])
        hT = sb("hT", [P, 2, FC, ET])
        ya = sb("ya", [P, ES, DM])
        yb = sb("yb", [P, EB, ES, DM])
        yi = sb("yi", [P, EB, ES], u32)
        ly = sb("ly", [P, 2, 2, LG, DM])
        lu, lg = (t[:].rearrange("p (t d) -> p t d", d=DM) for t in (t1, t2))
        lx, lo, ls = x4, xn4, xT4[:].rearrange("p b (t d) -> p b t d", d=DM)

        BK = [ctx.enter_context(nc.psum_tensor(f"bank{i}", [P, 512], f32)) for i in range(8)]
        BS, BST, BA, BB, BC = BK[0:4], BK[4], BK[5], BK[6], BK[7]

        block = ctx.enter_context(nc.Block())

        @block.sync
        def _(eng):
            def ln_load(n, b):
                eng.dma_start(x4[:, b], by_tile(x)[:, ds(n * LG, LG), :]).then_inc(sem(f"x_in{b}"), 16)

            eng.dma_start(tab[:, :FIRST], tables[:, :FIRST]).then_inc(sem("tables"), 16)
            for i, w in enumerate((WQ, WK, WV)):
                eng.dma_start(wrow[:, i, :], w.rearrange("h u d -> (h u) d")).then_inc(sem("weights"), 16)
            eng.dma_start(gwr[:], gate_w).then_inc(sem("weights"), 16)
            for b in range(LB):
                ln_load(b, b)
            eng.dma_start(gbb[:], gate_b.rearrange("(o e) -> o e", o=1).broadcast_to([P, NE])).then_inc(sem("weights"), 16)
            eng.dma_start(gcol[:, 0:1], gamma.rearrange("(p o) -> p o", o=1)).then_inc(sem("weights"), 16)
            eng.dma_start(gcol[:, 1:2], beta.rearrange("(p o) -> p o", o=1)).then_inc(sem("weights"), 16)
            eng.dma_start(wrow[:, 3, :], WO).then_inc(sem("weights"), 16)
            eng.dma_start(tab[:, FIRST:], tables[:, FIRST:]).then_inc(sem("step_tables"), 16)

            def ln_step(i, b, more=True):
                n = LB * i + b
                eng.wait_ge(sem("xn"), n + 1)
                eng.dma_start(by_tile(xn_d)[:, ds(n * LG, LG), :], xn4[:, b]).then_inc(sem(f"xn_out{b}"), 16)
                if more:
                    ln_load(n + LB, b)
                eng.wait_ge(sem("xT4"), n + 1)
                eng.dma_start(xnT_d[:, ds(n * LG * P, LG * P)], xT4[:, b]).then_inc(sem(f"xT_out{b}"), 16)

            def body(i):
                for b in range(LB):
                    ln_step(i, b)

            turns(eng, NLN // LB - 1, body)
            for b in range(LB):
                ln_step(NLN // LB - 1, b, False)
            for b in range(LB):
                eng.wait_ge(sem(f"xn_out{b}"), 16 * NLN // LB)
                eng.wait_ge(sem(f"xT_out{b}"), 16 * NLN // LB)

            def step_loads(i, off):
                m, par = QPS * i + off, off % 2
                if due(m - 1):
                    eng.wait_ge(sem("v"), m - 1)
                eng.dma_start(xin[:, par], xnT_d[:, ds(m * 2 * P, 2 * P)]).then_inc(sem(f"xin{par}"), 16)
                for a in range(4):
                    if due(16 * even(i, off)):
                        eng.wait_ge(sem(f"sent{par}{a}"), 16 * even(i, off))
                for k in range(TOPK):
                    eng.dma_start(rows[:, par, :, k, 0:DM], by_tile(xn_d)[:, ds(2 * m, 2), :]).then_inc(sem(f"rows{par}"), 16)

            def s_store(m, par):
                eng.wait_ge(sem("s_ev"), m + 1)
                eng.dma_start(by_tile(s_d)[:, ds(2 * m, 2), :], sout[:, par]).then_inc(sem(f"s_out{par}"), 16)

            step_loads(0, 0)
            step_loads(0, 1)

            eng.wait_ge(sem("zero"), 1)
            eng.wait_ge(sem("zt"), 1)
            with eng.Fori(0, NZ) as j:
                g = eng.value_load(zt[0:1, ds(j, 1)], min_val=0, max_val=NET + NZ - 1)
                eng.dma_start(xs_d[ds(g * ET, ET), :].rearrange("(s p) d -> p s d", p=P), zero[:]).then_inc(sem("xs_zeroed"), 16)

            def body(i):
                for q in range(QPS):
                    step_loads(i, q + 2)
                    s_store(QPS * i + q, q % 2)

            turns(eng, NPAIR // QPS - 1, body)
            for n in range(NPAIR - QPS, NPAIR):
                if n + 2 < NPAIR:
                    step_loads(0, n + 2)
                s_store(n, n % 2)
            for par in range(2):
                eng.wait_ge(sem(f"s_out{par}"), 16 * NPAIR // 2)
                for a in range(4):
                    eng.wait_ge(sem(f"sent{par}{a}"), 16 * NPAIR // 2)

            def tile_loads(i, b):
                g = EB * i + b
                if due(g - EB + 1):
                    eng.wait_ge(sem("xtp"), g - EB + 1)
                    eng.wait_ge(sem("mt"), g - EB + 1)
                eng.dma_start(xr[:, b], xs_d[ds(g * ET, ET), :].rearrange("(s p) d -> p s d", p=P)).then_inc(sem(f"xr{b}"), 16)
                e = eng.value_load(tmap[0:1, ds(g, 1)], min_val=0, max_val=NE - 1)
                if due(g - EB + 1):
                    eng.wait_ge(sem("h"), FC * (g - EB + 1))
                    eng.wait_ge(sem("ya"), g - EB + 1)
                eng.dma_start(wb[:, b], stage[:, ds(e, 1), :].rearrange("p o w -> p (o w)")).then_inc(sem(f"wb{b}"), 16)

            eng.wait_ge(sem("tmap"), 1)
            eng.wait_ge(sem("staged"), 16 * (2 + 2 * NE))

            def body(i):
                for b in range(EB):
                    tile_loads(i, b)

            turns(eng, NET // EB, body)

            for b in range(EB):
                for s in range(ES):
                    eng.wait_ge(sem(f"ys{b}{s}"), 16 * NET // EB)

            def last_loads(n, par):
                if due(n - 1):
                    eng.wait_ge(sem("l_used"), n - 1)
                for k in range(TOPK):
                    eng.dma_start(ly[:, par, k], by_tile(y_d)[:, ds(n * LG + k * NT, LG), :]).then_inc(sem(f"l_in{par}"), 16)
                eng.dma_start(ls[:, par], by_tile(s_d)[:, ds(n * LG, LG), :]).then_inc(sem(f"l_in{par}"), 16)
                eng.dma_start(lx[:, par], by_tile(x)[:, ds(n * LG, LG), :]).then_inc(sem(f"l_in{par}"), 16)

            def last_store(n, par):
                eng.wait_ge(sem("l_used"), n + 1)
                eng.dma_start(by_tile(out)[:, ds(n * LG, LG), :], lo[:, par]).then_inc(sem(f"l_out{par}"), 16)

            last_loads(0, 0)
            last_loads(1, 1)
            def body(i):
                for par in range(2):
                    last_store(2 * i + par, par)
                    last_loads(2 * i + par + 2, par)

            turns(eng, NT // (2 * LG) - 1, body)
            for par in range(2):
                last_store(NT // LG - 2 + par, par)
            for par in range(2):
                eng.wait_ge(sem(f"l_out{par}"), 16 * NT // (2 * LG))

        @block.gpsimd
        def _(eng):
            eng.memset(zero[:], 0.0).then_inc(sem("zero"), 1)
            eng.memset(slots[:, 0], 0.0).then_inc(sem("slots0"), 1)
            eng.memset(vexp[:], 0.0).then_inc(sem("slots0"), 1)
            eng.memset(slots[:, 1], 0.0).then_inc(sem("slots0"), 1)
            eng.wait_ge(sem("tables"), 16)
            eng.tensor_copy(ident16[:], ident).then_inc(sem("ident16"), 1)
            eng.wait_ge(sem("wmax"), 1)
            eng.partition_all_reduce(wmaxa[:], wmax[:], P, bass.bass_isa.ReduceOp.max).then_inc(sem("wmaxa"), 1)

            def feed(i, off):
                m, par = QPS * i + off, off % 2
                eng.wait_ge(sem("rot"), m + 1)
                if due(4 * (m - 1)):
                    eng.wait_ge(sem("kv"), 4 * (m - 1))
                eng.tensor_tensor(kst[:, par].rearrange("p a h d -> p (a h) d"),
                                  qf[:, par, 1, :].rearrange("p (n d) -> p n d", d=DH),
                                  T("kgrow").rearrange("p (q n o) -> p q n o", q=QPS, o=1)[:, off % QPS].broadcast_to([P, 2 * NH, DH]),
                                  ALU.mult).then_inc(sem("kst"), 1)
                eng.wait_ge(sem(f"rows{par}"), 32 * (even(i, off) + 1))
                eng.tensor_copy(rows[:, par].rearrange("p a k r -> p (a k) r")[:, :, DM:ROW],
                                meta[:, ds(2 * m, 2)].rearrange("p a k r -> p (a k) r")).then_inc(sem("meta_in"), 1)
                eng.tensor_copy(sidx[:, par], posu[:, ds(2 * m, 2)].rearrange("p a k -> p (a k)")).then_inc(sem("meta_in"), 1)
                eng.wait_ge(sem("meta_in"), 2 * (m + 1))
                eng.sem_inc(sem("meta_in_seen"), 1)
                for a in range(2):
                    for k in range(TOPK):
                        j = TOPK * a + k
                        eng.indirect_dma_start(xs_d, bass.IndirectOffsetOnAxis(ap=sidx[:, par, j:j + 1], axis=0),
                                               rows[:, par, a, k, :], None).then_inc(sem(f"sent{par}{j}"), 16)

            eng.wait_ge(sem("step_tables"), 16)
            eng.wait_ge(sem("meta"), 1)
            eng.wait_ge(sem("xs_zeroed"), 16 * NZ)
            feed(0, 0)
            def body(i):
                for q in range(QPS):
                    feed(i, q + 1)

            turns(eng, NPAIR // QPS - 1, body)
            for n in range(NPAIR - QPS, NPAIR - 1):
                feed(0, n + 1)

            def give(g, b):
                eng.wait_ge(sem("yb"), g + 1)
                eng.sem_inc(sem("yb_seen"), 1)
                for s in range(ES):
                    eng.indirect_dma_start(y_d, bass.IndirectOffsetOnAxis(ap=yi[:, b, s:s + 1], axis=0),
                                           yb[:, b, s, :], None, bounds_check=TOPK * TOK - 1,
                                           oob_is_err=False).then_inc(sem(f"ys{b}{s}"), 16)

            def body(i):
                for b in range(EB):
                    give(EB * i + b, b)

            turns(eng, NET // EB, body)

        @block.scalar
        def _(eng):
            def std(n, par):
                eng.wait_ge(sem("bn"), (LG + 1) * (n + 1))
                if due(n - 1):
                    eng.wait_ge(sem("lnr"), n - 1)
                eng.activation(std4[:, par], bmv[:, par, :, 1], ACT.Sqrt, bias=T("eps")).then_inc(sem("ln_std"), 1)

            def keep_transposed(i, b):
                eng.wait_ge(sem("ln_tp"), LB * i + b + 1)
                if due(16 * i):
                    eng.wait_ge(sem(f"xT_out{b}"), 16 * i)
                eng.activation(xT4[:, b], BS[b % 2][:], ACT.Copy).then_inc(sem("xT4"), 1)

            std(0, 0)
            def body(i, more=LB):
                for b in range(LB):
                    if b < more:
                        std(LB * i + b + 1, (b + 1) % 2)
                    keep_transposed(i, b)

            turns(eng, NLN // LB - 1, body)
            body(NLN // LB - 1, LB - 1)

            eng.dma_start(stage[:, :, 0:FF], w1.rearrange("e d f -> d e f")).then_inc(sem("staged"), 16)
            for e in range(NE):
                eng.dma_start(stage[:, e, FF:W1W], b1[e].rearrange("(c p) -> p c", p=P),
                              allow_slow_non_contiguous=True).then_inc(sem("staged"), 16)
                eng.dma_start(stage[:, e, W1W:W1W + FF].rearrange("p (c h) -> p c h", c=FC),
                              w2[e].rearrange("(c p) h -> p c h", p=P)).then_inc(sem("staged"), 16)
            eng.dma_start(stage[:, :, W1W + FF:WROW],
                          b2.rearrange("(o e) h -> o e h", o=1).broadcast_to([P, NE, DM])).then_inc(sem("staged"), 16)
            eng.wait_ge(sem("dm"), 1)
            eng.activation(ew[:], m2[:], ACT.Exp).then_inc(sem("ew"), 1)

            def front_h(m, par):
                eng.wait_ge(sem("rot"), m + 1)
                if due(2 * (m - 1)):
                    eng.wait_ge(sem("tp"), 2 * (m - 1))
                for qk, sl in ((0, slice(0, 2)), (1, slice(0, 3, 2))):
                    src = qf[:, par, qk, :].rearrange("p (n o d) -> p n o d", o=1, d=DH).broadcast_to([P, 2 * NH, 2, DH])
                    dst = slots[:, par, qk].rearrange("p a h s d -> p (a h) s d")[:, :, sl, :]
                    eng.activation(dst, src, ACT.Copy).then_inc(sem("hi"), 1)

            def v_ev(m, par):
                eng.wait_ge(sem("v"), m + 1)
                if due(m - 1):
                    eng.wait_ge(sem("R"), m - 1)
                for pr in range(2):
                    h = slice(CH * pr, CH * pr + CH)
                    eng.activation(vexp[h, par].rearrange("p c (m r d) -> p (c m) r d", r=2, d=DH)[:, :, pr, :],
                                   BA[h, 0:256].rearrange("p (n d) -> p n d", d=DH), ACT.Copy)
                eng.activation(vpl[:, par].rearrange("p a d -> p (a d)"), BA[:, 256:512], ACT.Copy).then_inc(sem("vexp"), 1)

            def tp_ev(m, par, a):
                eng.wait_ge(sem("tp"), 2 * m + a + 1)
                if a == 0:
                    if due(4 * (m - 1)):
                        eng.wait_ge(sem("sc"), 4 * (m - 1))
                bank = BS[a]
                eng.activation(qkT[:, par, a].rearrange("p k g t -> p (k g t)"),
                               bank[:].bitcast(f16), ACT.Copy).then_inc(sem("tp_ev"), 1)

            def slot(i, q, prev, back, front):
                n, par = QPS * i + q, (q + 1) % 2
                if back:
                    v_ev(n, 1 - par)
                if prev:
                    eng.wait_ge(sem("rt"), n)
                    if due(n - 1):
                        eng.wait_ge(sem("s"), n - 1)
                    eng.activation(rnT[:], BA[:, 0:256], ACT.Identity, bias=gcol[:, 1:2], scale=gcol[:, 0:1]).then_inc(sem("rnT"), 1)
                    eng.wait_ge(sem("s"), n)
                    if due(16 * even(i, q - 1)):
                        eng.wait_ge(sem(f"s_out{par}"), 16 * even(i, q - 1))
                    eng.activation(sout[:, par].rearrange("p a d -> p (a d)"), BA[:, 0:256], ACT.Copy).then_inc(sem("s_ev"), 1)
                if front:
                    front_h(n + 1, par)
                if back:
                    eng.wait_ge(sem("R"), n + 1)
                    if due(n):
                        eng.wait_ge(sem("gn"), n)
                    eng.activation(sqr[:], BC[:, 0:256], ACT.Square, scale=unscale[:, 0:1]).then_inc(sem("sqr"), 1)
                    eng.wait_ge(sem("gn"), n + 1)
                    if due(n):
                        eng.wait_ge(sem("rstd"), n)
                    eng.activation(rn_std[:], ssum[:], ACT.Sqrt, scale=1.0 / DH, bias=T("eps")).then_inc(sem("std"), 1)
                if front:
                    tp_ev(n + 1, par, 0)
                    tp_ev(n + 1, par, 1)
                    eng.wait_ge(sem("qt"), n + 2)
                    if due(n - 1 + 1):
                        eng.wait_ge(sem("R"), n)
                    eng.activation(qT[:, par], BS[3][:, 0:256], ACT.Copy).then_inc(sem("qT"), 1)

            eng.wait_ge(sem("scales"), 1)
            eng.wait_ge(sem("slots0"), 3)
            def body(i):
                for q in range(QPS):
                    slot(i, q, True, True, True)

            slot(-1, 3, False, False, True)
            for q in range(QPS):
                slot(0, q, q > 0, True, True)
            with eng.Fori(1, NPAIR // QPS - 1) as i:
                body(i)
            for q in range(QPS):
                slot(NPAIR // QPS - 1, q, True, True, q + 1 < QPS)
            slot(NPAIR // QPS, 0, True, False, False)

            def turn_in(g, par):
                eng.wait_ge(sem("xtp"), g + 1)
                if due(4 * (g - 1)):
                    eng.wait_ge(sem("l1"), 4 * (g - 1))
                eng.activation(xT[:, par], BST[:, 0:256], ACT.Copy).then_inc(sem("xT"), 1)

            def gelu(g, par, b):
                if due(g - 1):
                    eng.wait_ge(sem("l2"), g - 1)
                for c in range(FC):
                    eng.wait_ge(sem("l1"), FC * g + c + 1)
                    eng.activation(hT[:, par, c], BS[c][:, par * ET:(par + 1) * ET],
                                   ACT.Gelu, bias=wb[:, b, FF + c:FF + c + 1]).then_inc(sem("h"), 1)

            turn_in(0, 0)
            def body(i, more=EB):
                for b in range(EB):
                    if b < more:
                        turn_in(EB * i + b + 1, (b + 1) % 2)
                    gelu(EB * i + b, b % 2, b)

            turns(eng, NET // EB - 1, body)
            body(NET // EB - 1, EB - 1)

            def body(i):
                for par in range(2):
                    eng.wait_ge(sem("lu"), 2 * i + par + 1)
                    eng.activation(lg, lu, ACT.Silu).then_inc(sem("lg"), 1)

            turns(eng, NT // (2 * LG), body)

        @block.vector
        def _(eng):
            seq = [0]

            def step(ins):
                seq[0] += 1
                ins.then_inc(sem("dve_step"), 1)
                eng.wait_ge(sem("dve_step"), seq[0])

            eng.wait_ge(sem("weights"), 128)
            eng.wait_ge(sem("tables"), 16)
            step(eng.tensor_reduce(wmaxa[:], wrow[:, 0:2, :], AX.XY, ALU.max))
            step(eng.tensor_reduce(wmin[:], wrow[:, 0:2, :], AX.XY, ALU.min))
            eng.scalar_tensor_tensor(wmax[:], wmin[:], -1.0, wmaxa[:], ALU.mult, ALU.max).then_inc(sem("wmax"), 1)
            eng.wait_ge(sem("wtp"), 4)
            step(eng.tensor_reduce(vmean[:], BK[6][:, 0:DM].rearrange("p (h u) -> p h u", u=DH), AX.X, ALU.add))
            step(eng.tensor_scalar(vmean[:], vmean[:], 1.0 / DH, None, ALU.mult))
            step(eng.tensor_tensor(wvc[:].rearrange("p (h u) -> p h u", u=DH), BK[6][:, 0:DM].rearrange("p (h u) -> p h u", u=DH),
                                   vmean[:].rearrange("p (h o) -> p h o", o=1).broadcast_to([P, NH, DH]), ALU.subtract))
            eng.wait_ge(sem("wmaxa"), 1)
            step(eng.tensor_scalar(wmaxa[:], wmaxa[:], 1e-30, None, ALU.max))
            step(eng.tensor_scalar(wmaxa[:].bitcast(u32), wmaxa[:].bitcast(u32), 0x7F800000, None, ALU.bitwise_and))
            step(eng.reciprocal(sq_scale[:], wmaxa[:]))
            step(eng.tensor_scalar(sq_scale[:], sq_scale[:], 32.0, None, ALU.mult))
            step(eng.tensor_scalar(wmaxa[:], wmaxa[:], 1.0 / 32.0, None, ALU.mult))
            step(eng.tensor_tensor(unscale[:], wmaxa[:], wmaxa[:], ALU.mult))
            step(eng.tensor_tensor(gcol[:, 0:1], gcol[:, 0:1], unscale[:], ALU.mult))
            for pr in range(2):
                step(eng.tensor_copy(wvp[:, pr].rearrange("p (m d) -> p m d", d=DH), wvc[:].rearrange("p (m r d) -> p m r d", r=2, d=DH)[:, :, pr, :]))
            for qk in range(2):
                for gp in range(2):
                    step(eng.tensor_scalar(
                        wqk[:, qk, 64 * gp:64 * gp + 64].rearrange("p (r h u) -> p r h u", r=2, h=4),
                        BK[4 + qk][:, 64 * gp:64 * gp + 64].rearrange("p (h r u) -> p r h u", h=4, r=2),
                        sq_scale[:, 0:1], None, ALU.mult))
            eng.tensor_copy(gwT[:], BK[7][:, 0:NE]).then_inc(sem("scales"), 1)

            def gate_out(n, par):
                eng.wait_ge(sem("lgt"), n + 1)
                eng.tensor_tensor(logits[:, ds(n * LG, LG), :], BS[2 + par][:, 0:LG * NE].rearrange("p (t e) -> p t e", e=NE),
                                  gbb[:].rearrange("p (o e) -> p o e", o=1).broadcast_to([P, LG, NE]), ALU.add).then_inc(sem("logit"), 1)

            def stats(i, off):
                b = off % LB
                eng.wait_ge(sem(f"x_in{b}"), 16 * (i + off // LB + 1))
                for t in range(LG):
                    eng.bn_stats(bst[:, b % 2, t], x4[:, b, t]).then_inc(sem("bn"), 1)

            def moments(i, off):
                n = LB * i + off
                if due(n - 1):
                    eng.wait_ge(sem("xn"), n - 1)
                eng.wait_ge(sem("bn"), (LG + 1) * n + LG)
                eng.sem_inc(sem("bn_seen"), 1)
                for t in range(LG):
                    ins = eng.bn_aggr(bmv[:, off % 2, t], bst[:, off % 2, t])
                ins.then_inc(sem("bn"), 1)

            def ln_step(i, b, more=True):
                n, par = LB * i + b, b % 2
                if more:
                    stats(i, b + 1)
                eng.wait_ge(sem("ln_std"), n + 1)
                eng.reciprocal(rstd4[:, par], std4[:, par]).then_inc(sem("lnr"), 1)
                eng.wait_ge(sem("lnr"), n + 1)
                if due(16 * i):
                    eng.wait_ge(sem(f"xn_out{b}"), 16 * i)
                for t in range(LG):
                    ins = eng.tensor_scalar(xn4[:, b, t], x4[:, b, t], bmv[:, par, t, 0:1], rstd4[:, par, t:t + 1], ALU.subtract, ALU.mult)
                ins.then_inc(sem("xn"), 1)
                if more:
                    moments(i, b + 1)
                if due(n - 1):
                    gate_out(n - 2, par)

            stats(0, 0)
            moments(0, 0)
            def body(i):
                for b in range(LB):
                    ln_step(i, b)

            turns(eng, NLN // LB - 1, body)
            for b in range(LB):
                ln_step(NLN // LB - 1, b, b + 1 < LB)
            gate_out(NLN - 2, 0)
            gate_out(NLN - 1, 1)

            eng.wait_ge(sem("logit"), NLN)
            bc = lambda a: a.rearrange("p (t o) -> p t o", o=1).broadcast_to([P, NT, NE])
            rev = T("rev").rearrange("p (o e) -> p o e", o=1).broadcast_to([P, NT, NE])
            step(eng.tensor_reduce(m1[:], logits[:], AX.X, ALU.max))
            step(eng.tensor_tensor(ra[:], logits[:], bc(m1[:]), ALU.is_equal))
            step(eng.tensor_tensor(rb[:], ra[:], rev, ALU.mult))
            step(eng.tensor_reduce(mr[:], rb[:], AX.X, ALU.max))
            step(eng.tensor_tensor(oh1[:], rev, bc(mr[:]), ALU.is_equal))
            step(eng.scalar_tensor_tensor(ra[:], oh1[:], -BIG, logits[:], ALU.mult, ALU.add))
            step(eng.tensor_reduce(m2[:], ra[:], AX.X, ALU.max))
            step(eng.tensor_tensor(rb[:], ra[:], bc(m2[:]), ALU.is_equal))
            step(eng.tensor_tensor(ra[:], rb[:], rev, ALU.mult))
            step(eng.tensor_reduce(mr[:], ra[:], AX.X, ALU.max))
            step(eng.tensor_tensor(oh2[:], rev, bc(mr[:]), ALU.is_equal))
            step(eng.tensor_tensor(ra[:], oh1[:], oh2[:], ALU.add))
            eng.tensor_tensor(m2[:], m2[:], m1[:], ALU.subtract).then_inc(sem("dm"), 1)
            eng.wait_ge(sem("dm"), 1)
            eng.wait_ge(sem("cnt"), 1)
            step(eng.tensor_copy(cnt[:], BK[4][0:NT, 0:NE]))
            eng.tensor_tensor(cm[:], cnt[:].rearrange("p (o e) -> p o e", o=1).broadcast_to([NT, NT, NE]),
                                   T("tlt", NT).rearrange("p (t o) -> p t o", o=1).broadcast_to([NT, NT, NE]), ALU.mult).then_inc(sem("cm"), 1)
            eng.wait_ge(sem("rank"), 2)
            step(eng.tensor_scalar(tiles[:], BK[6][:, 0:NE], 1.0 / ET, (ET - 1.0) / ET - 0.5 + 0.5 / ET, ALU.mult, ALU.add))
            step(eng.tensor_scalar(tiles[:], tiles[:], MAGIC, None, ALU.add))
            step(eng.tensor_scalar(tiles[:], tiles[:], MAGIC, None, ALU.subtract))
            step(eng.tensor_tensor(tri[:], T("elt").rearrange("p (a b) -> p a b", b=NE),
                                   tiles[:].rearrange("p (o e) -> p o e", o=1).broadcast_to([P, NE, NE]), ALU.mult))
            step(eng.tensor_reduce(first[:], tri[:], AX.X, ALU.add))
            step(eng.tensor_tensor(last[:], first[:], tiles[:], ALU.add))
            step(eng.tensor_scalar(first[:], first[:], float(ET), None, ALU.mult))
            step(eng.tensor_scalar(zcand[:, 0:NE], last[0:1, :], 1.0, None, ALU.subtract))
            step(eng.tensor_scalar(zcand[:, NE:NZ], T("gidx", 1)[:, 0:NZ - NE], last[0:1, NE - 1:NE], None, ALU.add))
            step(eng.tensor_scalar(zok[:, 0:NE], tiles[0:1, :], 0.0, None, ALU.is_gt))
            step(eng.tensor_scalar(zok[:, NE:NZ], zcand[:, NE:NZ], float(NET), None, ALU.is_lt))
            step(eng.tensor_tensor(zcand[:], zcand[:], T("dump", 1), ALU.subtract))
            step(eng.tensor_tensor(zcand[:], zcand[:], zok[:], ALU.mult))
            eng.tensor_tensor(zt[:], zcand[:], T("dump", 1), ALU.add).then_inc(sem("zt"), 1)
            step(eng.tensor_tensor(rb[:], BK[5][:].rearrange("p (t e) -> p t e", e=NE),
                                   first[:].rearrange("p (o e) -> p o e", o=1).broadcast_to([P, NT, NE]), ALU.add))
            for k, oh in enumerate((oh1, oh2)):
                step(eng.tensor_tensor(ra[:], rb[:], oh[:], ALU.mult))
                step(eng.tensor_reduce(posf[:, :, k], ra[:], AX.X, ALU.add))
            step(eng.tensor_copy(posu[:], posf[:]))
            eng.wait_ge(sem("ew"), 1)
            step(eng.tensor_scalar(den[:], ew[:], 1.0, None, ALU.add))
            step(eng.memset(meta[:], 0.0))
            step(eng.reciprocal(meta[:, :, 0, 1], den[:]))
            step(eng.tensor_tensor(meta[:, :, 1, 1], ew[:], meta[:, :, 0, 1], ALU.mult))
            eng.tensor_copy(meta[:, :, :, 0], T("dest").rearrange("p (t k) -> p t k", k=TOPK)).then_inc(sem("meta"), 1)
            step(eng.tensor_tensor(tcmp[:], last[0:1, :].rearrange("p (o e) -> p o e", o=1).broadcast_to([1, NET, NE]),
                                   T("gidx", 1).rearrange("p (t o) -> p t o", o=1).broadcast_to([1, NET, NE]), ALU.is_le))
            step(eng.tensor_reduce(tmf[:], tcmp[:], AX.X, ALU.add))
            eng.tensor_scalar(tmap[:], tmf[:], float(NE - 1), None, ALU.min).then_inc(sem("tmap"), 1)

            eng.wait_ge(sem("step_tables"), 16)
            causal = T("causal").rearrange("p (o t) -> p o t", o=1).broadcast_to([P, 8, CH])
            smask, sdec = T("smask"), T("sdec")
            cosT = T("cos").rearrange("p (q w) -> p q w", q=QPS)
            sinT = T("sin").rearrange("p (q n two) -> p q n two", q=QPS, two=2)

            def state(n, q, c):
                if due(4 * n + c):
                    eng.wait_ge(sem("kv"), 4 * n + c)
                if q == 0 and c == 0:
                    ins = eng.memset(sg[:, 0], 0.0)
                else:
                    k = 4 * q + c
                    ins = eng.scalar_tensor_tensor(sg[:, c % 2], BST[:, 0:DM], sdec[:, k:k + 1], smask, ALU.mult, ALU.mult)
                ins.then_inc(sem("sg"), 1)

            def slot(i, q, prev, back, front):
                n, m, par, mq = QPS * i + q, QPS * i + q + 1, (q + 1) % 2, (q + 1) % QPS
                if back:
                    state(n, q, 0)
                    for hh in range(4):
                        eng.wait_ge(sem("sc"), 4 * n + hh + 1)
                        if due(n):
                            eng.wait_ge(sem("R"), n)
                        eng.tensor_tensor(prob[:, hh].rearrange("p (b t) -> p b t", t=CH), BS[hh][:].rearrange("p (b t) -> p b t", t=CH),
                                          causal, ALU.mult).then_inc(sem("prob"), 1)
                if front:
                    eng.wait_ge(sem("qk"), m + 1)
                    if due(m):
                        eng.wait_ge(sem("rot"), m)
                    eng.tensor_tensor(t1[:], BB[:], cosT[:, mq], ALU.mult).then_inc(sem("rot_part"), 1)
                if back:
                    state(n, q, 1)
                if front:
                    src = BB[:].rearrange("p (n two) -> p n two", two=2)
                    dst = t2[:].rearrange("p (n two) -> p n two", two=2)
                    for z in range(2):
                        eng.tensor_tensor(dst[:, :, z], src[:, :, 1 - z], sinT[:, mq, :, z], ALU.mult).then_inc(sem("rot_part"), 1)
                if back:
                    state(n, q, 2)
                if front:
                    eng.wait_ge(sem("rot_part"), 3 * (m + 1))
                    if due(m - 1):
                        eng.wait_ge(sem("qt"), m - 1)
                    if due(2 * (m - 1)):
                        eng.wait_ge(sem("hi"), 2 * (m - 1))
                    if due(m - 1):
                        eng.wait_ge(sem("kst"), m - 1)
                    eng.tensor_tensor(qf[:, par].rearrange("p k w -> p (k w)"), t1[:], t2[:], ALU.add).then_inc(sem("rot"), 1)
                if back:
                    state(n, q, 3)
                if front:
                    eng.wait_ge(sem("hi"), 2 * (m + 1))
                    for qk, sl in ((0, 2), (1, 1)):
                        s5 = slots[:, par, qk].rearrange("p a h s d -> p (a h) s d")
                        eng.wait_ge(sem("rot"), m + 1)
                        eng.tensor_tensor(s5[:, :, sl, :], qf[:, par, qk, :].rearrange("p (n d) -> p n d", d=DH), s5[:, :, 0, :],
                                          ALU.subtract).then_inc(sem("lo"), 1)
                if back:
                    eng.wait_ge(sem("sqr"), n + 1)
                    eng.tensor_reduce(ssum[:], sqr[:].rearrange("p (n d) -> p n d", d=DH), AX.X, ALU.add).then_inc(sem("gn"), 1)
                    eng.wait_ge(sem("std"), n + 1)
                    eng.reciprocal(ssum[:], rn_std[:]).then_inc(sem("rstd"), 1)
                    eng.wait_ge(sem("rstd"), n + 1)
                    if due(n):
                        eng.wait_ge(sem("rt"), n)
                    eng.tensor_tensor(rn[:].rearrange("p (n d) -> p n d", d=DH), BC[:, 0:256].rearrange("p (n d) -> p n d", d=DH),
                                      ssum[:].rearrange("p (n o) -> p n o", o=1).broadcast_to([P, 32, DH]), ALU.mult).then_inc(sem("rn"), 1)

            def body(i):
                for q in range(QPS):
                    slot(i, q, True, True, True)

            slot(-1, 3, False, False, True)
            for q in range(QPS):
                slot(0, q, q > 0, True, True)
            with eng.Fori(1, NPAIR // QPS - 1) as i:
                body(i)
            for q in range(QPS):
                slot(NPAIR // QPS - 1, q, True, True, q + 1 < QPS)
            slot(NPAIR // QPS, 0, True, False, False)

            def take_meta(i, off):
                g, b = EB * i + off, off % EB
                eng.wait_ge(sem(f"xr{b}"), 16 * (i + off // EB + 1))
                if due(g - EB + 1):
                    eng.wait_ge(sem("yb"), g - EB + 1)
                eng.tensor_copy(mt[:, b], xr[:, b, :, DM:DM + 2]).then_inc(sem("mt"), 1)

            def finish(i, b):
                g = EB * i + b
                for s in range(ES):
                    if due(16 * i):
                        eng.wait_ge(sem(f"ys{b}{s}"), 16 * i)
                eng.wait_ge(sem("mt"), g + 1)
                eng.tensor_scalar(yi[:, b], mt[:, b, :, 0], float(TOPK * TOK), None, ALU.add).then_inc(sem("yi"), 1)
                eng.wait_ge(sem("l2"), g + 1)
                eng.wait_ge(sem(f"wb{b}"), 16 * (i + 1))
                if due(g):
                    eng.wait_ge(sem("yb"), g)
                eng.tensor_tensor(ya[:], (BA, BB)[b % 2][:, 0:ET].rearrange("p (s d) -> p s d", d=DM),
                                  wb[:, b, W1W + FF:WROW].rearrange("p (o d) -> p o d", o=1).broadcast_to([P, ES, DM]),
                                  ALU.add).then_inc(sem("ya"), 1)
                eng.wait_ge(sem("ya"), g + 1)
                eng.wait_ge(sem("yi"), g + 1)
                eng.tensor_tensor(yb[:, b], ya[:], mt[:, b, :, 1:2].broadcast_to([P, ES, DM]), ALU.mult).then_inc(sem("yb"), 1)

            take_meta(0, 0)
            take_meta(0, 1)
            def body(i, more=EB):
                for b in range(EB):
                    finish(i, b)
                    if b < more:
                        take_meta(i, b + 2)

            turns(eng, NET // EB - 1, body)
            body(NET // EB - 1, EB - 2)

            def body(i):
                for par in range(2):
                    n = 2 * i + par
                    eng.wait_ge(sem(f"l_in{par}"), 64 * (i + 1))
                    if due(n):
                        eng.wait_ge(sem("lg"), n)
                    eng.tensor_tensor(lu, ly[:, par, 0], ly[:, par, 1], ALU.add).then_inc(sem("lu"), 1)
                    eng.wait_ge(sem("lg"), n + 1)
                    if due(16 * i):
                        eng.wait_ge(sem(f"l_out{par}"), 16 * i)
                    if due(n):
                        eng.wait_ge(sem("l_used"), n)
                    eng.tensor_tensor(ls[:, par], lg, ls[:, par], ALU.mult).then_inc(sem("lm"), 1)
                    eng.wait_ge(sem("lm"), n + 1)
                    eng.tensor_tensor(lo[:, par], lx[:, par], ls[:, par], ALU.add).then_inc(sem("l_used"), 1)

            turns(eng, NT // (2 * LG), body)

        @block.tensor
        def _(eng):
            mm = eng.matmul
            eng.wait_ge(sem("tables"), 16)
            eng.wait_ge(sem("weights"), 128)
            for j in range(3):
                eng.transpose(BK[4 + j][:, 0:DM], wrow[:, j, :], ident).then_inc(sem("wtp"), 1)
            eng.transpose(BK[7][:, 0:NE], gwr[:], ident[0:NE, 0:NE]).then_inc(sem("wtp"), 1)

            def logit(i, b):
                n, par = LB * i + b, b % 2
                eng.wait_ge(sem("xT4"), n + 1)
                if due(n - 1):
                    eng.wait_ge(sem("logit"), n - 1)
                for t in range(LG):
                    ins = mm(BS[2 + par][:, t * NE:(t + 1) * NE], xT4[:, b, t * P:(t + 1) * P], gwT[:], start=True, stop=True)
                ins.then_inc(sem("lgt"), 1)

            def turn_rows(n, b):
                eng.wait_ge(sem("xn"), n + 1)
                if due(n - 1):
                    eng.wait_ge(sem("xT4"), n - 1)
                for t in range(LG):
                    ins = eng.transpose(BS[b % 2][:, t * P:(t + 1) * P], xn4[:, b, t], ident)
                ins.then_inc(sem("ln_tp"), 1)

            eng.wait_ge(sem("scales"), 1)
            turn_rows(0, 0)
            def body(i, more=LB):
                for b in range(LB):
                    if b < more:
                        turn_rows(LB * i + b + 1, (b + 1) % LB)
                    logit(i, b)

            turns(eng, NLN // LB - 1, body)
            body(NLN // LB - 1, LB - 1)

            eng.wait_ge(sem("dm"), 1)
            for e in range(NE):
                ins = mm(BK[4][0:NT, e:e + 1], ra[:, :, e], ones[:, 0:1], start=True, stop=True)
            ins.then_inc(sem("cnt"), 1)
            mm(BK[5][:], T("before"), ra[:].rearrange("p t e -> p (t e)"), start=True, stop=False)
            eng.wait_ge(sem("cm"), 1)
            mm(BK[5][:], ones[0:NT, :], cm[:].rearrange("p t e -> p (t e)"), start=False, stop=True).then_inc(sem("rank"), 1)
            mm(BK[6][:, 0:NE], ones[0:NT, :], cnt[:], start=True, stop=True).then_inc(sem("rank"), 1)
            eng.wait_ge(sem("meta"), 1)

            def turn(m, par, a):
                bank = BS[a][:].bitcast(f16)
                eng.wait_ge(sem("lo"), 2 * (m + 1))
                eng.wait_ge(sem("hi"), 2 * (m + 1))
                for k in range(2):
                    for g in range(4):
                        j = 4 * k + g
                        ins = eng.transpose(bank[:, j * P:(j + 1) * P],
                                            slots[:, par, k, a].rearrange("p h s d -> p (h s d)")[:, g * P:(g + 1) * P], ident16[:])
                ins.then_inc(sem("tp"), 1)

            def slot(i, q, prev, back, front):
                n, m, par, bp = QPS * i + q, QPS * i + q + 1, (q + 1) % 2, q % 2
                if back:
                    eng.wait_ge(sem("tp_ev"), 2 * (n + 1))
                    if due(4 * n):
                        eng.wait_ge(sem("prob"), 4 * n)
                    for hh in range(4):
                        if hh == 3:
                            eng.wait_ge(sem("qT"), n + 1)
                        r = slice(32 * hh, 32 * hh + 32)
                        for c in range(4):
                            a, tk = c // 2, slice(CH * (c % 2), CH * (c % 2) + CH)
                            for g in range(4):
                                pr, gp = g % 2, g // 2
                                o = (c * 2 + gp) * CH
                                ins = mm(BS[hh][CH * pr:CH * pr + CH, o:o + CH], qkT[r, bp, a, 1, g, tk], qkT[r, bp, a, 0, g, tk],
                                         start=True, stop=True)
                        ins.then_inc(sem("sc"), 1)
                if prev:
                    eng.wait_ge(sem("rn"), n)
                    eng.wait_ge(sem("vexp"), n + 1 if back else n)
                    for a in range(2):
                        ins = eng.transpose(BA[:, a * P:(a + 1) * P], rn[:, a * DM:(a + 1) * DM], ident)
                    ins.then_inc(sem("rt"), 1)
                if front:
                    eng.wait_ge(sem(f"xin{par}"), 16 * (even(i, q + 1) + 1))
                    for a in range(2):
                        ins = mm(BB[:].rearrange("p (k a d) -> p k a d", k=2, a=2)[:, :, a, :], xin[:, par, a * P:(a + 1) * P],
                                 wqk[:].rearrange("p k d -> p (k d)"), start=True, stop=True)
                    ins.then_inc(sem("qk"), 1)
                if prev:
                    eng.wait_ge(sem("rnT"), n)
                    for a in range(2):
                        ins = mm(BA[:, a * DM:(a + 1) * DM], rnT[:, a * P:(a + 1) * P], wrow[:, 3, :], start=True, stop=True)
                    ins.then_inc(sem("s"), 1)
                if back:
                    eng.wait_ge(sem("kst"), n + 1)
                    eng.wait_ge(sem("qT"), n + 1)
                    eng.wait_ge(sem("vexp"), n + 1)
                    for c in range(4):
                        a, h0 = c // 2, CH * (c % 2)
                        tk = slice(h0, h0 + CH)
                        eng.wait_ge(sem("sg"), 4 * n + c + 1)
                        mm(BST[:, 0:DM], kst[tk, bp, a].rearrange("p h d -> p (h d)"), vpl[tk, bp, a],
                           start=(q == 0 and c == 0), stop=True, skip_group_check=True).then_inc(sem("kv"), 1)
                        mm(BC[tk, a * DM:(a + 1) * DM], qT[:, bp, c * CH:(c + 1) * CH], sg[:, c % 2], start=True, stop=False, skip_group_check=True)
                        if c == 0:
                            eng.wait_ge(sem("prob"), 4 * (n + 1))
                        for pair in range(NH // 2):
                            gp, hh = pair // 4, pair % 4
                            o = (c * 2 + gp) * CH
                            v0 = 2 * DH * pair
                            ins = mm(BC[tk, a * DM + v0:a * DM + v0 + 2 * DH], prob[:, hh, o:o + CH], vexp[:, bp, c, v0:v0 + 2 * DH],
                                     start=False, stop=(pair == NH // 2 - 1), skip_group_check=True)
                    ins.then_inc(sem("R"), 1)
                if front:
                    turn(m, par, 0)
                    turn(m, par, 1)
                    for a in range(2):
                        ins = eng.transpose(BS[3][:, a * P:(a + 1) * P], qf[:, par, 0, a * DM:(a + 1) * DM], ident)
                    ins.then_inc(sem("qt"), 1)
                    if due(n):
                        eng.wait_ge(sem("s_ev"), n)
                    for c in range(4):
                        for pr in range(2):
                            mm(BA[CH * pr:CH * pr + CH, c * CH:(c + 1) * CH], xin[:, par, c * CH:(c + 1) * CH], wvp[:, pr, :],
                               start=True, stop=True)
                    for a in range(2):
                        ins = mm(BA[:, 256 + a * DM:256 + (a + 1) * DM], xin[:, par, a * P:(a + 1) * P], wvc[:], start=True, stop=True)
                    ins.then_inc(sem("v"), 1)

            def body(i):
                for q in range(QPS):
                    slot(i, q, True, True, True)

            slot(-1, 3, False, False, True)
            for q in range(QPS):
                slot(0, q, q > 0, True, True)
            with eng.Fori(1, NPAIR // QPS - 1) as i:
                body(i)
            for q in range(QPS):
                slot(NPAIR // QPS - 1, q, True, True, q + 1 < QPS)
            slot(NPAIR // QPS, 0, True, False, False)
            eng.wait_ge(sem("s_ev"), NPAIR)
            eng.wait_ge(sem("tp_ev"), 2 * NPAIR)

            def turn_rows(i, off):
                g, b = EB * i + off, off % EB
                eng.wait_ge(sem(f"xr{b}"), 16 * (i + off // EB + 1))
                if due(g):
                    eng.wait_ge(sem("xT"), g)
                for s in range(ES):
                    ins = eng.transpose(BST[:, s * P:(s + 1) * P], xr[:, b, s, 0:DM], ident)
                ins.then_inc(sem("xtp"), 1)

            def layer1(i, off):
                g, par, b = EB * i + off, off % 2, off % EB
                eng.wait_ge(sem("xT"), g + 1)
                eng.wait_ge(sem(f"wb{b}"), 16 * (i + off // EB + 1))
                for c in range(FC):
                    if due(FC * (g - 1) + c + 1):
                        eng.wait_ge(sem("h"), FC * (g - 1) + c + 1)
                    mm(BS[c][:, par * ET:(par + 1) * ET], wb[:, b, c * P:(c + 1) * P], xT[:, par], start=True, stop=True).then_inc(sem("l1"), 1)

            def layer2(i, b):
                g, par, bank = EB * i + b, b % 2, (BA, BB)[b % 2]
                if due(g):
                    eng.wait_ge(sem("ya"), g)
                eng.wait_ge(sem("h"), FC * (g + 1))
                for s in range(ES):
                    for c in range(FC):
                        ins = mm(bank[:, s * DM:(s + 1) * DM], hT[:, par, c, s * P:(s + 1) * P],
                                 wb[:, b, W1W + c * DM:W1W + (c + 1) * DM], start=(c == 0), stop=(c == FC - 1))
                ins.then_inc(sem("l2"), 1)

            turn_rows(0, 0)
            layer1(0, 0)
            turn_rows(0, 1)
            def body(i, ahead=2 * EB):
                for b in range(EB):
                    if b + 1 < ahead:
                        layer1(i, b + 1)
                    if b + 2 < ahead:
                        turn_rows(i, b + 2)
                    layer2(i, b)

            turns(eng, NET // EB - 1, body)
            body(NET // EB - 1, EB)


NAMES = ("x", "WQ", "WK", "WV", "WO", "gamma", "beta")
FFN_NAMES = ("gate_w", "gate_b", "w1", "b1", "w2", "b2")


def kernel(**inputs):
    from concourse import bacc
    from concourse.bass_utils import run_bass_kernel_spmd

    nc = bacc.Bacc("TRN2", target_bir_lowering=False, num_devices=1)
    arrays = {f"in_{n}": np.ascontiguousarray(inputs[f"L0_attn_{n}"]) for n in NAMES}
    arrays.update({f"in_{n}": np.ascontiguousarray(inputs[f"L0_ffn_{n}"]) for n in FFN_NAMES})
    arrays["in_x"] = arrays["in_x"].reshape(TOK, DM)
    arrays["tables"], at = constants()
    args = [nc.dram_tensor(n, a.shape, mybir.dt.from_np(a.dtype), kind="ExternalInput").ap() for n, a in arrays.items()]
    out = nc.dram_tensor("out", (TOK, DM), mybir.dt.float32, kind="ExternalOutput").ap()
    moe_retention(nc, *args, out, at)
    r = run_bass_kernel_spmd(nc, [arrays], core_ids=[0])
    return np.asarray(r.results[0]["out"]).reshape(NSEQ, SEQ, DM)
```

```python
import numpy as np
import concourse.bass as bass
from concourse import mybir
from contextlib import ExitStack

NSEQ, SEQ, DM = 8, 1024, 128
NH, DH = 16, 8
NE, FF, TOPK = 8, 512, 2
P = 128
TOK = NSEQ * SEQ
NT = TOK // P
FC = FF // P
CH = 64
EPS = 1e-5
ET = 256
ES = ET // P
EB = 4
NET = -(-((TOK * TOPK + NE * (ET - 1)) // ET) // EB) * EB
ROW = DM + 4
W1W, W2W = FF + FC, FF + DM
WROW = W1W + W2W
LG = 4
LB = 4
NLN = NT // LG
NZ = NE + NET - TOK * TOPK // ET
NPAIR = NT // 2
QPS = SEQ // (2 * P)

BIG = 3.0e38
MAGIC = float(2 ** 23)


def head_of(f):
    gp, par, hh = f // 64, (f // 32) % 2, (f // 8) % 4
    return 8 * gp + 2 * hh + par


def constants():
    f32 = np.float32
    c = {}
    part = np.arange(P)
    gam = 1.0 - 2.0 ** (-5.0 - np.arange(NH, dtype=np.float64))
    feat = np.arange(DM)
    hf = np.array([head_of(f) for f in feat])
    dim = feat % DH
    angle = (10.0 ** (-4.0 * (np.arange(0, DH, 2, dtype=f32) / f32(DH)))).astype(f32)
    pos = np.arange(SEQ, dtype=f32)
    nang = (pos[:, None] * angle[None, :]).astype(f32).astype(np.float64)
    cos, sin = np.cos(nang), np.sin(nang)
    ct = np.zeros((P, QPS, 2, 2, DM)); st = np.zeros_like(ct); kg = np.zeros((P, QPS, 2, NH))
    blk = hf[::DH]
    for q in range(QPS):
        for a in range(2):
            ps = (2 * q + a) * P + part
            rel = (ps % CH) - CH // 2
            for qk, sgn in ((0, 1.0), (1, -1.0)):
                dec = gam[hf][None, :] ** (sgn * rel[:, None])
                ct[:, q, qk, a] = cos[ps][:, dim // 2] * dec
                st[:, q, qk, a] = sin[ps][:, dim // 2] * dec * np.where(dim % 2 == 0, -1.0, 1.0)
            kg[:, q, a] = gam[blk][None, :] ** (-1.0 * CH * (ps // CH)[:, None])
    c["cos"], c["sin"] = ct.reshape(P, -1), st.reshape(P, -1)
    c["kgrow"] = kg.reshape(P, -1)
    c["sdec"] = gam[hf][:, None] ** (1.0 * CH * np.arange(SEQ // CH)[None, :])
    c["smask"] = hf[:, None] == (feat // DH)[None, :]
    c["causal"] = np.arange(CH)[None, :] >= (part % CH)[:, None]
    c["ident"] = np.eye(P)
    c["before"] = part[:, None] < part[None, :]
    c["ones"] = np.ones((P, P))
    c["tlt"] = part[:, None] < np.arange(NT)[None, :]
    c["eps"] = np.full((P, 1), EPS)
    c["rev"] = np.broadcast_to(NE - np.arange(NE), (P, NE))
    c["elt"] = np.broadcast_to((np.arange(NE)[None, :] < np.arange(NE)[:, None]).reshape(1, -1), (P, NE * NE))
    tok = np.arange(NT)[None, :] * P + part[:, None]
    c["dest"] = np.stack([tok - TOPK * TOK, tok + TOK - TOPK * TOK], -1).reshape(P, -1)
    c["gidx"] = np.broadcast_to(np.arange(NET), (P, NET))
    c["dump"] = np.broadcast_to(NET + np.arange(NZ), (P, NZ))
    late = ("cos", "sin", "kgrow", "sdec", "smask", "causal")
    c = {n: c[n] for n in sorted(c, key=lambda n: n in late)}
    at, off = {}, 0
    for n, a in c.items():
        at[n] = (off, a.shape[1]); off += a.shape[1]
    return np.concatenate([np.asarray(a, f32) for a in c.values()], 1).astype(f32), at


def moe_retention(nc, x, WQ, WK, WV, WO, gamma, beta, gate_w, gate_b, w1, b1, w2, b2, tables, out, AT):
    f32, f16, u32, i32 = mybir.dt.float32, mybir.dt.float16, mybir.dt.uint32, mybir.dt.int32
    ALU, ACT, AX = mybir.AluOpType, mybir.ActivationFunctionType, mybir.AxisListType
    ds = bass.ds
    ctx = ExitStack()
    sb = lambda n, s, d=f32: ctx.enter_context(nc.sbuf_tensor(n, s, d))
    dram = lambda n, s: nc.dram_tensor(n, s, f32, kind="Internal").ap()
    sems = {}

    def sem(n):
        if n not in sems:
            sems[n] = ctx.enter_context(nc.semaphore(n))
        return sems[n]

    def due(v):
        return not isinstance(v, int) or v > 0

    def even(i, off):
        return 2 * i + off // 2

    def places(arena):
        at = [0]

        def place(*dims, dtype=f32):
            words = int(np.prod(dims)) * (2 if dtype == f16 else 4) // 4
            flat = arena[:, at[0]:at[0] + words]
            at[0] += words
            names = "abcdefg"[:len(dims)]
            return (flat if dtype == f32 else flat.bitcast(dtype)).rearrange(
                f"p ({' '.join(names)}) -> p {' '.join(names)}", **dict(zip(names, dims)))
        return place

    xn_d = dram("xn_d", (TOK, DM))
    xnT_d = dram("xnT_d", (P, TOK))
    xs_d = dram("xs_d", ((NET + NZ) * ET, ROW))
    y_d = dram("y_d", (TOPK * TOK, DM))

    def by_tile(a):
        return a.rearrange("(t p) d -> p t d", p=P)

    def by_tile_of(a):
        return a[:].rearrange("p (t d) -> p t d", d=DM)

    def turns(eng, count, body):
        body(0)
        with eng.Fori(1, count) as i:
            body(i)

    with ctx:
        tab = sb("tab", [P, tables.shape[1]])

        def T(n, p=P):
            o, w = AT[n]
            return tab[0:p, o:o + w]

        FIRST = AT["cos"][0]
        ident, ones = T("ident"), T("ones")
        ident16 = sb("ident16", [P, P], f16)
        wrow = sb("wrow", [P, 4, DM])
        wqk = sb("wqk", [P, 2, DM])
        wvc = sb("wvc", [P, DM])
        wvp = sb("wvp", [P, 2, CH])
        gwr = sb("gwr", [NE, DM])
        gwT = sb("gwT", [P, NE])
        gbb = sb("gbb", [P, NE])
        gcol = sb("gcol", [P, 2])
        stage = sb("stage", [P, NE, WROW])
        zero = sb("zero", [P, ES, ROW])
        work = sb("work", [P, EB * WROW + EB * ES * ROW + 2 * ET + 2 * FC * ET + ES * DM + EB * ES * DM])
        xall = sb("xall", [P, NT * DM])
        s_all = sb("s_all", [P, NT, DM])
        place = places(work)
        x4, xn4, xT4 = place(LB, LG, DM), place(LB, LG, DM), place(LB, LG * P)
        bst = sb("bst", [P, 2, LG, 6])
        bmv = sb("bmv", [P, 2, LG, 2])
        std4 = sb("std4", [P, 2, LG])
        rstd4 = sb("rstd4", [P, 2, LG])
        logits = sb("logits", [P, NT, NE])
        oh1, oh2, ra, rb = (place(NT, NE) for _ in range(4))
        m1 = sb("m1", [P, NT]); m2 = sb("m2", [P, NT]); mr = sb("mr", [P, NT])
        ew = sb("ew", [P, NT]); den = sb("den", [P, NT])
        cnt = sb("cnt", [NT, NE]); cm = place(NT, NE)[0:NT]
        tiles = sb("tiles", [P, NE]); first = sb("first", [P, NE]); last = sb("last", [P, NE])
        tri = sb("tri", [P, NE, NE])
        posf = sb("posf", [P, NT, TOPK])
        posu = sb("posu", [P, NT, TOPK], u32)
        meta = sb("meta", [P, NT, TOPK, ROW - DM])
        tcmp = place(NET, NE)[0:1]; tmf = sb("tmf", [1, NET]); tmap = sb("tmap", [1, NET], i32)
        zcand = sb("zcand", [1, NZ]); zok = sb("zok", [1, NZ]); zt = sb("zt", [1, NZ], i32)
        wmin = sb("wmin", [P, 1]); wmax = sb("wmax", [P, 1]); wmaxa = sb("wmaxa", [P, 1])
        sq_scale = sb("sq_scale", [P, 1]); unscale = sb("unscale", [P, 1]); vmean = sb("vmean", [P, NH])
        xin = sb("xin", [P, QPS, 2 * P])
        t1 = sb("t1", [P, 512]); t2 = sb("t2", [P, 512])
        place = places(xall)
        prob = place(4, 512)
        qkT = place(2, 2, 2, 4, P, dtype=f16)
        qf = place(2, 2, 2 * DM)
        slots = place(2, 2, 2, NH, 4, DH, dtype=f16)
        vexp = place(2, 4, DM)
        vpl = sb("vpl", [P, 2, 2, DM])
        kst = sb("kst", [P, 2, 2, NH, DH])
        qT = sb("qT", [P, 2, 2 * P])
        sg = sb("sg", [P, 2, DM])
        sqr = sb("sqr", [P, 2 * DM]); ssum = sb("ssum", [P, 32]); rn_std = sb("rn_std", [P, 32])
        rn = sb("rn", [P, 2 * DM]); rnT = sb("rnT", [P, 2 * P])
        rows = sb("rows", [P, 2, 2, TOPK, ROW])
        sidx = sb("sidx", [P, 2, 2 * TOPK], u32)
        place = places(work)
        wb = place(EB, WROW)
        xr = place(EB, ES, ROW)
        xT = place(2, ET)
        hT = place(2, FC, ET)
        ya = place(ES, DM)
        yb = place(EB, ES, DM)
        mt = sb("mt", [P, EB, ES, 2])
        yi = sb("yi", [P, EB, ES], u32)
        place = places(work)
        ly = place(LB, TOPK, LG, DM)
        lo = place(LB, LG, DM)
        lu, lg = place(2, LG, DM), place(2, LG, DM)

        BK = [ctx.enter_context(nc.psum_tensor(f"bank{i}", [P, 512], f32)) for i in range(8)]
        BS, BST, BA, BB, BC = BK[0:4], BK[4], BK[5], BK[6], BK[7]

        block = ctx.enter_context(nc.Block())

        @block.sync
        def _(eng):
            def ln_load(n, b):
                eng.dma_start(x4[:, b], by_tile(x)[:, ds(n * LG, LG), :]).then_inc(sem(f"x_in{b}"), 16)

            eng.dma_start(tab[:, :FIRST], tables[:, :FIRST]).then_inc(sem("tables"), 16)
            for i, w in enumerate((WQ, WK, WV)):
                eng.dma_start(wrow[:, i, :], w.rearrange("h u d -> (h u) d")).then_inc(sem("weights"), 16)
            eng.dma_start(gwr[:], gate_w).then_inc(sem("weights"), 16)
            for b in range(LB):
                ln_load(b, b)
            eng.dma_start(gbb[:], gate_b.rearrange("(o e) -> o e", o=1).broadcast_to([P, NE])).then_inc(sem("weights"), 16)
            eng.dma_start(gcol[:, 0:1], gamma.rearrange("(p o) -> p o", o=1)).then_inc(sem("weights"), 16)
            eng.dma_start(gcol[:, 1:2], beta.rearrange("(p o) -> p o", o=1)).then_inc(sem("weights"), 16)
            eng.dma_start(wrow[:, 3, :], WO).then_inc(sem("weights"), 16)
            eng.dma_start(tab[:, FIRST:], tables[:, FIRST:]).then_inc(sem("step_tables"), 16)

            def ln_step(i, b, more=True):
                n = LB * i + b
                eng.wait_ge(sem("normalised"), n + 1)
                eng.dma_start(by_tile(xn_d)[:, ds(n * LG, LG), :], xn4[:, b]).then_inc(sem(f"xn_stored{b}"), 16)
                if more:
                    ln_load(n + LB, b)
                eng.wait_ge(sem("xn_T_kept"), n + 1)
                eng.dma_start(xnT_d[:, ds(n * LG * P, LG * P)], xT4[:, b]).then_inc(sem(f"xn_T_stored{b}"), 16)

            def body(i):
                for b in range(LB):
                    ln_step(i, b)

            turns(eng, NLN // LB - 1, body)
            for b in range(LB):
                ln_step(NLN // LB - 1, b, False)
            for b in range(LB):
                eng.wait_ge(sem(f"xn_stored{b}"), 16 * NLN // LB)
                eng.wait_ge(sem(f"xn_T_stored{b}"), 16 * NLN // LB)

            def turned_in(i, q):
                m = QPS * i + q
                if due(m - QPS + 1):
                    eng.wait_ge(sem("v_projected"), m - QPS + 1)
                eng.dma_start(xin[:, q], xnT_d[:, ds(m * 2 * P, 2 * P)]).then_inc(sem(f"xn_T_in{q}"), 16)

            def rows_in(i, off):
                m, par = QPS * i + off, off % 2
                for a in range(4):
                    if due(16 * even(i, off)):
                        eng.wait_ge(sem(f"rows_sent{par}{a}"), 16 * even(i, off))
                for k in range(TOPK):
                    eng.dma_start(rows[:, par, :, k, 0:DM], by_tile(xn_d)[:, ds(2 * m, 2), :]).then_inc(sem(f"rows_in{par}"), 16)

            for q in range(QPS):
                turned_in(0, q)
            rows_in(0, 0)
            rows_in(0, 1)

            eng.wait_ge(sem("zeros_ready"), 1)
            eng.wait_ge(sem("zero_tiles"), 1)
            with eng.Fori(0, NZ) as j:
                g = eng.value_load(zt[0:1, ds(j, 1)], min_val=0, max_val=NET + NZ - 1)
                eng.dma_start(xs_d[ds(g * ET, ET), :].rearrange("(s p) d -> p s d", p=P), zero[:]).then_inc(sem("xs_zeroed"), 16)


            for q in range(QPS):
                turned_in(1, q)
                rows_in(0, q + 2)
                if q == 1:
                    eng.dma_start(stage[:, :, 0:FF], w1.rearrange("e d f -> d e f")).then_inc(sem("staged"), 16)
                    for e in range(NE):
                        eng.dma_start(stage[:, e, FF:W1W], b1[e].rearrange("(c p) -> p c", p=P),
                                      allow_slow_non_contiguous=True).then_inc(sem("staged"), 16)
                        eng.dma_start(stage[:, e, W1W:W1W + FF].rearrange("p (c h) -> p c h", c=FC),
                                      w2[e].rearrange("(c p) h -> p c h", p=P)).then_inc(sem("staged"), 16)
                    eng.dma_start(stage[:, :, W1W + FF:WROW],
                                  b2.rearrange("(o e) h -> o e h", o=1).broadcast_to([P, NE, DM])).then_inc(sem("staged"), 16)
            with eng.Fori(1, NPAIR // QPS - 1) as i:
                for q in range(QPS):
                    turned_in(i + 1, q)
                    rows_in(i, q + 2)
            for q in range(QPS - 2):
                rows_in(NPAIR // QPS - 1, q + 2)
            for par in range(2):
                for a in range(4):
                    eng.wait_ge(sem(f"rows_sent{par}{a}"), 16 * NPAIR // 2)

            def tile_loads(i, b):
                g = EB * i + b
                if due(g - EB + 1):
                    eng.wait_ge(sem("rows_turned"), g - EB + 1)
                    eng.wait_ge(sem("meta_kept"), g - EB + 1)
                eng.dma_start(xr[:, b], xs_d[ds(g * ET, ET), :].rearrange("(s p) d -> p s d", p=P)).then_inc(sem(f"rows_read{b}"), 16)
                e = eng.value_load(tmap[0:1, ds(g, 1)], min_val=0, max_val=NE - 1)
                if due(g - EB + 1):
                    eng.wait_ge(sem("hidden"), FC * (g - EB + 1))
                    eng.wait_ge(sem("biased"), g - EB + 1)
                eng.dma_start(wb[:, b], stage[:, ds(e, 1), :].rearrange("p o w -> p (o w)")).then_inc(sem(f"expert_weights{b}"), 16)

            eng.wait_ge(sem("tile_experts"), 1)
            eng.wait_ge(sem("staged"), 16 * (2 + 2 * NE))

            for b in range(EB):
                tile_loads(0, b)
            eng.wait_ge(sem("s_kept"), NPAIR)
            with eng.Fori(1, NLN + 1) as i:
                for b in range(EB):
                    tile_loads(i, b)
                eng.dma_start(by_tile_of(xall)[:, ds((i - 1) * LG, LG), :], by_tile(x)[:, ds((i - 1) * LG, LG), :]).then_inc(sem("x_again"), 16)
            for i in range(NLN + 1, NET // EB):
                for b in range(EB):
                    tile_loads(i, b)

            for b in range(EB):
                for s in range(ES):
                    eng.wait_ge(sem(f"results_sent{b}{s}"), 16 * NET // EB)

            def last_loads(i, b):
                n = LB * i + b
                if due(n - LB + 1):
                    eng.wait_ge(sem("experts_added"), n - LB + 1)
                for k in range(TOPK):
                    eng.dma_start(ly[:, b, k], by_tile(y_d)[:, ds(n * LG + k * NT, LG), :]).then_inc(sem(f"results_in{b}"), 16)

            def last_store(n, b):
                eng.wait_ge(sem("out_kept"), n + 1)
                eng.dma_start(by_tile(out)[:, ds(n * LG, LG), :], lo[:, b]).then_inc(sem(f"out_stored{b}"), 16)

            for b in range(LB):
                last_loads(0, b)

            def body(i):
                for b in range(LB):
                    last_store(LB * i + b, b)
                    last_loads(i + 1, b)

            turns(eng, NLN // LB - 1, body)
            for b in range(LB):
                last_store(NLN - LB + b, b)
            for b in range(LB):
                eng.wait_ge(sem(f"out_stored{b}"), 16 * NLN // LB)

        @block.gpsimd
        def _(eng):
            eng.memset(zero[:], 0.0).then_inc(sem("zeros_ready"), 1)
            eng.memset(slots[:, 0], 0.0).then_inc(sem("pads_zeroed"), 1)
            eng.memset(vexp[:], 0.0).then_inc(sem("pads_zeroed"), 1)
            eng.memset(slots[:, 1], 0.0).then_inc(sem("pads_zeroed"), 1)
            eng.wait_ge(sem("tables"), 16)
            eng.tensor_copy(ident16[:], ident).then_inc(sem("ident16"), 1)
            eng.wait_ge(sem("wmax"), 1)
            eng.partition_all_reduce(wmaxa[:], wmax[:], P, bass.bass_isa.ReduceOp.max).then_inc(sem("wmaxa"), 1)

            def decay(i, off):
                m, par = QPS * i + off, off % 2
                eng.wait_ge(sem("positions_applied"), m + 1)
                if due(4 * (m - 1)):
                    eng.wait_ge(sem("chunk_in_state"), 4 * (m - 1))
                eng.tensor_tensor(kst[:, par].rearrange("p a h d -> p (a h) d"),
                                  qf[:, par, 1, :].rearrange("p (n d) -> p n d", d=DH),
                                  T("kgrow").rearrange("p (q n o) -> p q n o", q=QPS, o=1)[:, off % QPS].broadcast_to([P, 2 * NH, DH]),
                                  ALU.mult).then_inc(sem("k_decayed"), 1)

            def send(i, q):
                n, par = QPS * i + q, q % 2
                eng.wait_ge(sem(f"rows_in{par}"), 32 * (even(i, q) + 1))
                eng.tensor_copy(rows[:, par].rearrange("p a k r -> p (a k) r")[:, :, DM:ROW],
                                meta[:, ds(2 * n, 2)].rearrange("p a k r -> p (a k) r")).then_inc(sem("rows_complete"), 1)
                eng.tensor_copy(sidx[:, par], posu[:, ds(2 * n, 2)].rearrange("p a k -> p (a k)")).then_inc(sem("rows_complete"), 1)
                eng.wait_ge(sem("rows_complete"), 2 * (n + 1))
                eng.sem_inc(sem("rows_complete_seen"), 1)
                for a in range(2):
                    for k in range(TOPK):
                        j = TOPK * a + k
                        eng.indirect_dma_start(xs_d, bass.IndirectOffsetOnAxis(ap=sidx[:, par, j:j + 1], axis=0),
                                               rows[:, par, a, k, :], None).then_inc(sem(f"rows_sent{par}{j}"), 16)

            eng.wait_ge(sem("step_tables"), 16)
            for q in range(3):
                decay(0, q)
            eng.wait_ge(sem("meta"), 1)
            eng.wait_ge(sem("xs_zeroed"), 16 * NZ)
            def body(i):
                for q in range(QPS):
                    send(i, q)
                    decay(i, q + 3)

            turns(eng, NPAIR // QPS - 1, body)
            for q in range(QPS):
                send(NPAIR // QPS - 1, q)
                if q + 3 < QPS:
                    decay(NPAIR // QPS - 1, q + 3)

            def give(g, b):
                eng.wait_ge(sem("weighted"), g + 1)
                eng.sem_inc(sem("weighted_seen"), 1)
                for s in range(ES):
                    eng.indirect_dma_start(y_d, bass.IndirectOffsetOnAxis(ap=yi[:, b, s:s + 1], axis=0),
                                           yb[:, b, s, :], None, bounds_check=TOPK * TOK - 1,
                                           oob_is_err=False).then_inc(sem(f"results_sent{b}{s}"), 16)

            def body(i):
                for b in range(EB):
                    give(EB * i + b, b)

            turns(eng, NET // EB, body)

        @block.scalar
        def _(eng):
            def std(n, par):
                eng.wait_ge(sem("moments"), (LG + 1) * (n + 1))
                if due(n - 1):
                    eng.wait_ge(sem("ln_rstd"), n - 1)
                eng.activation(std4[:, par], bmv[:, par, :, 1], ACT.Sqrt, bias=T("eps")).then_inc(sem("ln_std"), 1)

            def keep_transposed(i, b):
                eng.wait_ge(sem("xn_turned"), LB * i + b + 1)
                if due(16 * i):
                    eng.wait_ge(sem(f"xn_T_stored{b}"), 16 * i)
                eng.activation(xT4[:, b], BS[b % 2][:], ACT.Copy).then_inc(sem("xn_T_kept"), 1)

            std(0, 0)
            def body(i, more=LB):
                for b in range(LB):
                    if b < more:
                        std(LB * i + b + 1, (b + 1) % 2)
                    keep_transposed(i, b)

            turns(eng, NLN // LB - 1, body)
            body(NLN // LB - 1, LB - 1)

            def front_h(m, par):
                eng.wait_ge(sem("positions_applied"), m + 1)
                if due(2 * (m - 1)):
                    eng.wait_ge(sem("slots_turned"), 2 * (m - 1))
                for qk, sl in ((0, slice(0, 2)), (1, slice(0, 3, 2))):
                    src = qf[:, par, qk, :].rearrange("p (n o d) -> p n o d", o=1, d=DH).broadcast_to([P, 2 * NH, 2, DH])
                    dst = slots[:, par, qk].rearrange("p a h s d -> p (a h) s d")[:, :, sl, :]
                    eng.activation(dst, src, ACT.Copy).then_inc(sem("high_halves"), 1)

            def v_ev(m, par):
                eng.wait_ge(sem("v_projected"), m + 1)
                if due(m - 1):
                    eng.wait_ge(sem("retained"), m - 1)
                for pr in range(2):
                    h = slice(CH * pr, CH * pr + CH)
                    eng.activation(vexp[h, par].rearrange("p c (m r d) -> p (c m) r d", r=2, d=DH)[:, :, pr, :],
                                   BA[h, 0:256].rearrange("p (n d) -> p n d", d=DH), ACT.Copy)
                eng.activation(vpl[:, par].rearrange("p a d -> p (a d)"), BA[:, 256:512], ACT.Copy).then_inc(sem("v_kept"), 1)

            def tp_ev(m, par, a):
                eng.wait_ge(sem("slots_turned"), 2 * m + a + 1)
                if a == 0:
                    if due(4 * (m - 1)):
                        eng.wait_ge(sem("scores"), 4 * (m - 1))
                bank = BS[a]
                eng.activation(qkT[:, par, a].rearrange("p k g t -> p (k g t)"),
                               bank[:].bitcast(f16), ACT.Copy).then_inc(sem("slots_kept"), 1)

            def slot(i, q, prev, back, front):
                n, par = QPS * i + q, (q + 1) % 2
                if back:
                    v_ev(n, 1 - par)
                if prev:
                    eng.wait_ge(sem("rn_turned"), n)
                    if due(n - 1):
                        eng.wait_ge(sem("through_wo"), n - 1)
                    eng.activation(rnT[:], BA[:, 0:256], ACT.Identity, bias=gcol[:, 1:2], scale=gcol[:, 0:1]).then_inc(sem("rn_T_kept"), 1)
                    eng.wait_ge(sem("through_wo"), n)
                    eng.activation(s_all[:, ds(2 * (n - 1), 2), :].rearrange("p a d -> p (a d)"), BA[:, 0:256], ACT.Copy).then_inc(sem("s_kept"), 1)
                if front:
                    front_h(n + 1, par)
                if back:
                    eng.wait_ge(sem("retained"), n + 1)
                    if due(n):
                        eng.wait_ge(sem("squares_summed"), n)
                    eng.activation(sqr[:], BC[:, 0:256], ACT.Square, scale=unscale[:, 0:1]).then_inc(sem("squares"), 1)
                    eng.wait_ge(sem("squares_summed"), n + 1)
                    if due(n):
                        eng.wait_ge(sem("gn_rstd"), n)
                    eng.activation(rn_std[:], ssum[:], ACT.Sqrt, scale=1.0 / DH, bias=T("eps")).then_inc(sem("gn_std"), 1)
                if front:
                    tp_ev(n + 1, par, 0)
                    tp_ev(n + 1, par, 1)
                    eng.wait_ge(sem("q_turned"), n + 2)
                    if due(n):
                        eng.wait_ge(sem("retained"), n)
                    eng.activation(qT[:, par], BS[3][:, 0:256], ACT.Copy).then_inc(sem("q_T_kept"), 1)

            eng.wait_ge(sem("scales"), 1)
            eng.wait_ge(sem("pads_zeroed"), 3)
            def body(i):
                for q in range(QPS):
                    slot(i, q, True, True, True)

            slot(-1, 3, False, False, True)
            eng.wait_ge(sem("choices"), 1)
            eng.activation(ew[:], m2[:], ACT.Exp).then_inc(sem("exp_kept"), 1)
            for q in range(QPS):
                slot(0, q, q > 0, True, True)
            with eng.Fori(1, NPAIR // QPS - 1) as i:
                body(i)
            for q in range(QPS):
                slot(NPAIR // QPS - 1, q, True, True, q + 1 < QPS)
            slot(NPAIR // QPS, 0, True, False, False)

            def turn_in(g, par):
                eng.wait_ge(sem("rows_turned"), g + 1)
                if due(4 * (g - 1)):
                    eng.wait_ge(sem("layer1"), 4 * (g - 1))
                eng.activation(xT[:, par], BST[:, 0:256], ACT.Copy).then_inc(sem("rows_T_kept"), 1)

            def gelu(g, par, b):
                if due(g - 1):
                    eng.wait_ge(sem("layer2"), g - 1)
                for c in range(FC):
                    eng.wait_ge(sem("layer1"), FC * g + c + 1)
                    eng.activation(hT[:, par, c], BS[c][:, par * ET:(par + 1) * ET],
                                   ACT.Gelu, bias=wb[:, b, FF + c:FF + c + 1]).then_inc(sem("hidden"), 1)

            turn_in(0, 0)
            def body(i, more=EB):
                for b in range(EB):
                    if b < more:
                        turn_in(EB * i + b + 1, (b + 1) % 2)
                    gelu(EB * i + b, b % 2, b)

            turns(eng, NET // EB - 1, body)
            body(NET // EB - 1, EB - 1)

            def body(i):
                for b in range(LB):
                    n, par = LB * i + b, b % 2
                    eng.wait_ge(sem("experts_added"), n + 1)
                    if due(n - 1):
                        eng.wait_ge(sem("s_times_silu"), n - 1)
                    eng.activation(lg[:, par], lu[:, par], ACT.Silu).then_inc(sem("silu_kept"), 1)

            turns(eng, NLN // LB, body)

        @block.vector
        def _(eng):
            seq = [0]

            def step(ins):
                seq[0] += 1
                ins.then_inc(sem("dve_step"), 1)
                eng.wait_ge(sem("dve_step"), seq[0])

            eng.wait_ge(sem("weights"), 128)
            eng.wait_ge(sem("tables"), 16)
            step(eng.tensor_reduce(wmaxa[:], wrow[:, 0:2, :], AX.XY, ALU.max))
            step(eng.tensor_reduce(wmin[:], wrow[:, 0:2, :], AX.XY, ALU.min))
            eng.scalar_tensor_tensor(wmax[:], wmin[:], -1.0, wmaxa[:], ALU.mult, ALU.max).then_inc(sem("wmax"), 1)
            eng.wait_ge(sem("weights_turned"), 4)
            eng.tensor_copy(gwT[:], BK[7][:, 0:NE]).then_inc(sem("gate_w"), 1)

            def gate_out(n, par):
                eng.wait_ge(sem("gate_product"), n + 1)
                eng.tensor_tensor(logits[:, ds(n * LG, LG), :], BS[2 + par][:, 0:LG * NE].rearrange("p (t e) -> p t e", e=NE),
                                  gbb[:].rearrange("p (o e) -> p o e", o=1).broadcast_to([P, LG, NE]), ALU.add).then_inc(sem("logits_kept"), 1)

            def stats(i, off):
                b = off % LB
                eng.wait_ge(sem(f"x_in{b}"), 16 * (i + off // LB + 1))
                for t in range(LG):
                    eng.bn_stats(bst[:, b % 2, t], x4[:, b, t]).then_inc(sem("moments"), 1)

            def moments(i, off):
                n = LB * i + off
                if due(n - 1):
                    eng.wait_ge(sem("normalised"), n - 1)
                eng.wait_ge(sem("moments"), (LG + 1) * n + LG)
                eng.sem_inc(sem("moments_seen"), 1)
                for t in range(LG):
                    ins = eng.bn_aggr(bmv[:, off % 2, t], bst[:, off % 2, t])
                ins.then_inc(sem("moments"), 1)

            def ln_step(i, b, more=True):
                n, par = LB * i + b, b % 2
                if more:
                    stats(i, b + 1)
                eng.wait_ge(sem("ln_std"), n + 1)
                eng.reciprocal(rstd4[:, par], std4[:, par]).then_inc(sem("ln_rstd"), 1)
                eng.wait_ge(sem("ln_rstd"), n + 1)
                if due(16 * i):
                    eng.wait_ge(sem(f"xn_stored{b}"), 16 * i)
                for t in range(LG):
                    ins = eng.tensor_scalar(xn4[:, b, t], x4[:, b, t], bmv[:, par, t, 0:1], rstd4[:, par, t:t + 1], ALU.subtract, ALU.mult)
                ins.then_inc(sem("normalised"), 1)
                if more:
                    moments(i, b + 1)
                if due(n - 1):
                    gate_out(n - 2, par)

            stats(0, 0)
            moments(0, 0)
            def body(i):
                for b in range(LB):
                    ln_step(i, b)

            turns(eng, NLN // LB - 1, body)
            for b in range(LB):
                ln_step(NLN // LB - 1, b, b + 1 < LB)
            step(eng.tensor_reduce(vmean[:], BK[6][:, 0:DM].rearrange("p (h u) -> p h u", u=DH), AX.X, ALU.add))
            step(eng.tensor_scalar(vmean[:], vmean[:], 1.0 / DH, None, ALU.mult))
            step(eng.tensor_tensor(wvc[:].rearrange("p (h u) -> p h u", u=DH), BK[6][:, 0:DM].rearrange("p (h u) -> p h u", u=DH),
                                   vmean[:].rearrange("p (h o) -> p h o", o=1).broadcast_to([P, NH, DH]), ALU.subtract))
            eng.wait_ge(sem("wmaxa"), 1)
            step(eng.tensor_scalar(wmaxa[:], wmaxa[:], 1e-30, None, ALU.max))
            step(eng.tensor_scalar(wmaxa[:].bitcast(u32), wmaxa[:].bitcast(u32), 0x7F800000, None, ALU.bitwise_and))
            step(eng.reciprocal(sq_scale[:], wmaxa[:]))
            step(eng.tensor_scalar(sq_scale[:], sq_scale[:], 32.0, None, ALU.mult))
            step(eng.tensor_scalar(wmaxa[:], wmaxa[:], 1.0 / 32.0, None, ALU.mult))
            step(eng.tensor_tensor(unscale[:], wmaxa[:], wmaxa[:], ALU.mult))
            step(eng.tensor_tensor(gcol[:, 0:1], gcol[:, 0:1], unscale[:], ALU.mult))
            for pr in range(2):
                step(eng.tensor_copy(wvp[:, pr].rearrange("p (m d) -> p m d", d=DH), wvc[:].rearrange("p (m r d) -> p m r d", r=2, d=DH)[:, :, pr, :]))
            for qk in range(2):
                for gp in range(2):
                    step(eng.tensor_scalar(
                        wqk[:, qk, 64 * gp:64 * gp + 64].rearrange("p (r h u) -> p r h u", r=2, h=4),
                        BK[4 + qk][:, 64 * gp:64 * gp + 64].rearrange("p (h r u) -> p r h u", h=4, r=2),
                        sq_scale[:, 0:1], None, ALU.mult))
            eng.sem_inc(sem("scales"), 1)
            gate_out(NLN - 2, 0)
            gate_out(NLN - 1, 1)

            def choose():
                eng.wait_ge(sem("logits_kept"), NLN)
                bc = lambda a: a.rearrange("p (t o) -> p t o", o=1).broadcast_to([P, NT, NE])
                rev = T("rev").rearrange("p (o e) -> p o e", o=1).broadcast_to([P, NT, NE])
                step(eng.tensor_reduce(m1[:], logits[:], AX.X, ALU.max))
                step(eng.tensor_tensor(ra[:], logits[:], bc(m1[:]), ALU.is_equal))
                step(eng.tensor_tensor(rb[:], ra[:], rev, ALU.mult))
                step(eng.tensor_reduce(mr[:], rb[:], AX.X, ALU.max))
                step(eng.tensor_tensor(oh1[:], rev, bc(mr[:]), ALU.is_equal))
                step(eng.scalar_tensor_tensor(ra[:], oh1[:], -BIG, logits[:], ALU.mult, ALU.add))
                step(eng.tensor_reduce(m2[:], ra[:], AX.X, ALU.max))
                step(eng.tensor_tensor(rb[:], ra[:], bc(m2[:]), ALU.is_equal))
                step(eng.tensor_tensor(ra[:], rb[:], rev, ALU.mult))
                step(eng.tensor_reduce(mr[:], ra[:], AX.X, ALU.max))
                step(eng.tensor_tensor(oh2[:], rev, bc(mr[:]), ALU.is_equal))
                step(eng.tensor_tensor(ra[:], oh1[:], oh2[:], ALU.add))
                eng.tensor_tensor(m2[:], m2[:], m1[:], ALU.subtract).then_inc(sem("choices"), 1)
                eng.wait_ge(sem("choices"), 1)
                eng.wait_ge(sem("counts"), 1)
                step(eng.tensor_copy(cnt[:], BST[0:NT, 0:NE]))
                eng.tensor_tensor(cm[:], cnt[:].rearrange("p (o e) -> p o e", o=1).broadcast_to([NT, NT, NE]),
                                       T("tlt", NT).rearrange("p (t o) -> p t o", o=1).broadcast_to([NT, NT, NE]), ALU.mult).then_inc(sem("counts_before"), 1)
                eng.wait_ge(sem("totals"), 1)
                step(eng.tensor_scalar(tiles[:], BST[:, 0:NE], 1.0 / ET, (ET - 1.0) / ET - 0.5 + 0.5 / ET, ALU.mult, ALU.add))
                step(eng.tensor_scalar(tiles[:], tiles[:], MAGIC, None, ALU.add))
                step(eng.tensor_scalar(tiles[:], tiles[:], MAGIC, None, ALU.subtract))
                step(eng.tensor_tensor(tri[:], T("elt").rearrange("p (a b) -> p a b", b=NE),
                                       tiles[:].rearrange("p (o e) -> p o e", o=1).broadcast_to([P, NE, NE]), ALU.mult))
                step(eng.tensor_reduce(first[:], tri[:], AX.X, ALU.add))
                step(eng.tensor_tensor(last[:], first[:], tiles[:], ALU.add))
                step(eng.tensor_scalar(first[:], first[:], float(ET), None, ALU.mult))

            def rank_rows():
                eng.wait_ge(sem("rank"), 1)
                eng.tensor_tensor(rb[:], BA[:].rearrange("p (t e) -> p t e", e=NE),
                                       first[:].rearrange("p (o e) -> p o e", o=1).broadcast_to([P, NT, NE]), ALU.add).then_inc(sem("ranked"), 1)

            def route():
                step(eng.tensor_scalar(zcand[:, 0:NE], last[0:1, :], 1.0, None, ALU.subtract))
                step(eng.tensor_scalar(zcand[:, NE:NZ], T("gidx", 1)[:, 0:NZ - NE], last[0:1, NE - 1:NE], None, ALU.add))
                step(eng.tensor_scalar(zok[:, 0:NE], tiles[0:1, :], 0.0, None, ALU.is_gt))
                step(eng.tensor_scalar(zok[:, NE:NZ], zcand[:, NE:NZ], float(NET), None, ALU.is_lt))
                step(eng.tensor_tensor(zcand[:], zcand[:], T("dump", 1), ALU.subtract))
                step(eng.tensor_tensor(zcand[:], zcand[:], zok[:], ALU.mult))
                eng.tensor_tensor(zt[:], zcand[:], T("dump", 1), ALU.add).then_inc(sem("zero_tiles"), 1)
                eng.wait_ge(sem("ranked"), 1)
                for k, oh in enumerate((oh1, oh2)):
                    step(eng.tensor_tensor(ra[:], rb[:], oh[:], ALU.mult))
                    step(eng.tensor_reduce(posf[:, :, k], ra[:], AX.X, ALU.add))
                step(eng.tensor_copy(posu[:], posf[:]))
                eng.wait_ge(sem("exp_kept"), 1)
                step(eng.tensor_scalar(den[:], ew[:], 1.0, None, ALU.add))
                step(eng.memset(meta[:], 0.0))
                step(eng.reciprocal(meta[:, :, 0, 1], den[:]))
                step(eng.tensor_tensor(meta[:, :, 1, 1], ew[:], meta[:, :, 0, 1], ALU.mult))
                eng.tensor_copy(meta[:, :, :, 0], T("dest").rearrange("p (t k) -> p t k", k=TOPK)).then_inc(sem("meta"), 1)

            def tile_experts():
                step(eng.tensor_tensor(tcmp[:], last[0:1, :].rearrange("p (o e) -> p o e", o=1).broadcast_to([1, NET, NE]),
                                       T("gidx", 1).rearrange("p (t o) -> p t o", o=1).broadcast_to([1, NET, NE]), ALU.is_le))
                step(eng.tensor_reduce(tmf[:], tcmp[:], AX.X, ALU.add))
                eng.tensor_scalar(tmap[:], tmf[:], float(NE - 1), None, ALU.min).then_inc(sem("tile_experts"), 1)

            eng.wait_ge(sem("step_tables"), 16)
            causal = T("causal").rearrange("p (o t) -> p o t", o=1).broadcast_to([P, 8, CH])
            smask, sdec = T("smask"), T("sdec")
            cosT = T("cos").rearrange("p (q w) -> p q w", q=QPS)
            sinT = T("sin").rearrange("p (q n two) -> p q n two", q=QPS, two=2)

            def state(n, q, c):
                if due(4 * n + c):
                    eng.wait_ge(sem("chunk_in_state"), 4 * n + c)
                if q == 0 and c == 0:
                    ins = eng.memset(sg[:, 0], 0.0)
                else:
                    k = 4 * q + c
                    ins = eng.scalar_tensor_tensor(sg[:, c % 2], BST[:, 0:DM], sdec[:, k:k + 1], smask, ALU.mult, ALU.mult)
                ins.then_inc(sem("state_kept"), 1)

            def slot(i, q, prev, back, front):
                n, m, par, mq = QPS * i + q, QPS * i + q + 1, (q + 1) % 2, (q + 1) % QPS
                if back:
                    state(n, q, 0)
                if front:
                    eng.wait_ge(sem("qk_projected"), m + 1)
                    if due(m):
                        eng.wait_ge(sem("positions_applied"), m)
                    eng.tensor_tensor(t1[:], BB[:], cosT[:, mq], ALU.mult).then_inc(sem("position_parts"), 1)
                if back:
                    for hh in range(4):
                        eng.wait_ge(sem("scores"), 4 * n + hh + 1)
                        if due(n):
                            eng.wait_ge(sem("retained"), n)
                        eng.tensor_tensor(prob[:, hh].rearrange("p (b t) -> p b t", t=CH), BS[hh][:].rearrange("p (b t) -> p b t", t=CH),
                                          causal, ALU.mult).then_inc(sem("scores_masked"), 1)
                if back and not prev:
                    rank_rows()
                if back:
                    state(n, q, 1)
                if front:
                    src = BB[:].rearrange("p (n two) -> p n two", two=2)
                    dst = t2[:].rearrange("p (n two) -> p n two", two=2)
                    for z in range(2):
                        eng.tensor_tensor(dst[:, :, z], src[:, :, 1 - z], sinT[:, mq, :, z], ALU.mult).then_inc(sem("position_parts"), 1)
                if front:
                    eng.wait_ge(sem("position_parts"), 3 * (m + 1))
                    if due(m - 1):
                        eng.wait_ge(sem("q_turned"), m - 1)
                    if due(2 * (m - 1)):
                        eng.wait_ge(sem("high_halves"), 2 * (m - 1))
                    if due(m - 1):
                        eng.wait_ge(sem("k_decayed"), m - 1)
                    eng.tensor_tensor(qf[:, par].rearrange("p k w -> p (k w)"), t1[:], t2[:], ALU.add).then_inc(sem("positions_applied"), 1)
                if back:
                    state(n, q, 2)
                    state(n, q, 3)
                if front:
                    eng.wait_ge(sem("high_halves"), 2 * (m + 1))
                    for qk, sl in ((0, 2), (1, 1)):
                        s5 = slots[:, par, qk].rearrange("p a h s d -> p (a h) s d")
                        eng.wait_ge(sem("positions_applied"), m + 1)
                        eng.tensor_tensor(s5[:, :, sl, :], qf[:, par, qk, :].rearrange("p (n d) -> p n d", d=DH), s5[:, :, 0, :],
                                          ALU.subtract).then_inc(sem("low_halves"), 1)
                if back:
                    eng.wait_ge(sem("squares"), n + 1)
                    eng.tensor_reduce(ssum[:], sqr[:].rearrange("p (n d) -> p n d", d=DH), AX.X, ALU.add).then_inc(sem("squares_summed"), 1)
                    eng.wait_ge(sem("gn_std"), n + 1)
                    eng.reciprocal(ssum[:], rn_std[:]).then_inc(sem("gn_rstd"), 1)
                    eng.wait_ge(sem("gn_rstd"), n + 1)
                    if due(n):
                        eng.wait_ge(sem("rn_turned"), n)
                    eng.tensor_tensor(rn[:].rearrange("p (n d) -> p n d", d=DH), BC[:, 0:256].rearrange("p (n d) -> p n d", d=DH),
                                      ssum[:].rearrange("p (n o) -> p n o", o=1).broadcast_to([P, 32, DH]), ALU.mult).then_inc(sem("rn_kept"), 1)

            def body(i):
                for q in range(QPS):
                    slot(i, q, True, True, True)

            slot(-1, 3, False, False, True)
            choose()
            slot(0, 0, False, True, True)
            route()
            slot(0, 1, True, True, True)
            tile_experts()
            for q in range(2, QPS):
                slot(0, q, True, True, True)
            with eng.Fori(1, NPAIR // QPS - 1) as i:
                body(i)
            for q in range(QPS):
                slot(NPAIR // QPS - 1, q, True, True, q + 1 < QPS)
            slot(NPAIR // QPS, 0, True, False, False)

            def take_meta(i, off):
                g, b = EB * i + off, off % EB
                eng.wait_ge(sem(f"rows_read{b}"), 16 * (i + off // EB + 1))
                if due(g - EB + 1):
                    eng.wait_ge(sem("weighted"), g - EB + 1)
                eng.tensor_copy(mt[:, b], xr[:, b, :, DM:DM + 2]).then_inc(sem("meta_kept"), 1)

            def finish(i, b):
                g = EB * i + b
                for s in range(ES):
                    if due(16 * i):
                        eng.wait_ge(sem(f"results_sent{b}{s}"), 16 * i)
                eng.wait_ge(sem("meta_kept"), g + 1)
                eng.tensor_scalar(yi[:, b], mt[:, b, :, 0], float(TOPK * TOK), None, ALU.add).then_inc(sem("dest_kept"), 1)
                eng.wait_ge(sem("layer2"), g + 1)
                eng.wait_ge(sem(f"expert_weights{b}"), 16 * (i + 1))
                if due(g):
                    eng.wait_ge(sem("weighted"), g)
                eng.tensor_tensor(ya[:], (BA, BB)[b % 2][:, 0:ET].rearrange("p (s d) -> p s d", d=DM),
                                  wb[:, b, W1W + FF:WROW].rearrange("p (o d) -> p o d", o=1).broadcast_to([P, ES, DM]),
                                  ALU.add).then_inc(sem("biased"), 1)
                eng.wait_ge(sem("biased"), g + 1)
                eng.wait_ge(sem("dest_kept"), g + 1)
                eng.tensor_tensor(yb[:, b], ya[:], mt[:, b, :, 1:2].broadcast_to([P, ES, DM]), ALU.mult).then_inc(sem("weighted"), 1)

            take_meta(0, 0)
            take_meta(0, 1)
            def body(i, more=EB):
                for b in range(EB):
                    finish(i, b)
                    if b < more:
                        take_meta(i, b + 2)

            turns(eng, NET // EB - 1, body)
            body(NET // EB - 1, EB - 2)

            def add_experts(i, off):
                n, b, par = LB * i + off, off % LB, off % 2
                eng.wait_ge(sem(f"results_in{b}"), 16 * TOPK * (i + off // LB + 1))
                if due(n - 1):
                    eng.wait_ge(sem("silu_kept"), n - 1)
                eng.tensor_tensor(lu[:, par], ly[:, b, 0], ly[:, b, 1], ALU.add).then_inc(sem("experts_added"), 1)

            def add_in(i, b, more=True):
                n, par = LB * i + b, b % 2
                if more:
                    add_experts(i, b + 1)
                t = ds(n * LG, LG)
                eng.wait_ge(sem("silu_kept"), n + 1)
                eng.tensor_tensor(s_all[:, t, :], lg[:, par], s_all[:, t, :], ALU.mult).then_inc(sem("s_times_silu"), 1)
                eng.wait_ge(sem("s_times_silu"), n + 1)
                if due(16 * i):
                    eng.wait_ge(sem(f"out_stored{b}"), 16 * i)
                eng.tensor_tensor(lo[:, b], by_tile_of(xall)[:, t, :], s_all[:, t, :], ALU.add).then_inc(sem("out_kept"), 1)

            eng.wait_ge(sem("x_again"), 16 * NLN)
            add_experts(0, 0)
            def body(i):
                for b in range(LB):
                    add_in(i, b)

            turns(eng, NLN // LB - 1, body)
            for b in range(LB):
                add_in(NLN // LB - 1, b, b + 1 < LB)

        @block.tensor
        def _(eng):
            mm = eng.matmul
            eng.wait_ge(sem("tables"), 16)
            eng.wait_ge(sem("weights"), 128)
            for j in range(3):
                eng.transpose(BK[4 + j][:, 0:DM], wrow[:, j, :], ident).then_inc(sem("weights_turned"), 1)
            eng.transpose(BK[7][:, 0:NE], gwr[:], ident[0:NE, 0:NE]).then_inc(sem("weights_turned"), 1)

            def logit(i, b):
                n, par = LB * i + b, b % 2
                eng.wait_ge(sem("xn_T_kept"), n + 1)
                if due(n - 1):
                    eng.wait_ge(sem("logits_kept"), n - 1)
                for t in range(LG):
                    ins = mm(BS[2 + par][:, t * NE:(t + 1) * NE], xT4[:, b, t * P:(t + 1) * P], gwT[:], start=True, stop=True)
                ins.then_inc(sem("gate_product"), 1)

            def turn_rows(n, b):
                eng.wait_ge(sem("normalised"), n + 1)
                if due(n - 1):
                    eng.wait_ge(sem("xn_T_kept"), n - 1)
                for t in range(LG):
                    ins = eng.transpose(BS[b % 2][:, t * P:(t + 1) * P], xn4[:, b, t], ident)
                ins.then_inc(sem("xn_turned"), 1)

            turn_rows(0, 0)
            eng.wait_ge(sem("gate_w"), 1)
            def body(i, more=LB):
                for b in range(LB):
                    if b < more:
                        turn_rows(LB * i + b + 1, (b + 1) % LB)
                    logit(i, b)

            turns(eng, NLN // LB - 1, body)
            body(NLN // LB - 1, LB - 1)

            def turn(m, par, a):
                bank = BS[a][:].bitcast(f16)
                eng.wait_ge(sem("low_halves"), 2 * (m + 1))
                eng.wait_ge(sem("high_halves"), 2 * (m + 1))
                for k in range(2):
                    for g in range(4):
                        j = 4 * k + g
                        ins = eng.transpose(bank[:, j * P:(j + 1) * P],
                                            slots[:, par, k, a].rearrange("p h s d -> p (h s d)")[:, g * P:(g + 1) * P], ident16[:])
                ins.then_inc(sem("slots_turned"), 1)

            def project_qk(i, off):
                m, q = QPS * i + off, off % QPS
                eng.wait_ge(sem(f"xn_T_in{q}"), 16 * (i + off // QPS + 1))
                if due(3 * m):
                    eng.wait_ge(sem("position_parts"), 3 * m)
                for a in range(2):
                    ins = mm(BB[:].rearrange("p (k a d) -> p k a d", k=2, a=2)[:, :, a, :], xin[:, q, a * P:(a + 1) * P],
                             wqk[:].rearrange("p k d -> p (k d)"), start=True, stop=True)
                ins.then_inc(sem("qk_projected"), 1)

            def spread_v(mq, c):
                for pr in range(2):
                    mm(BA[CH * pr:CH * pr + CH, c * CH:(c + 1) * CH], xin[:, mq, c * CH:(c + 1) * CH], wvp[:, pr, :],
                       start=True, stop=True)

            def scores(n, bp, hh):
                if hh == 3:
                    eng.wait_ge(sem("q_T_kept"), n + 1)
                r = slice(32 * hh, 32 * hh + 32)
                for c in range(4):
                    a, tk = c // 2, slice(CH * (c % 2), CH * (c % 2) + CH)
                    for g in range(4):
                        pr, gp = g % 2, g // 2
                        o = (c * 2 + gp) * CH
                        ins = mm(BS[hh][CH * pr:CH * pr + CH, o:o + CH], qkT[r, bp, a, 1, g, tk], qkT[r, bp, a, 0, g, tk],
                                 start=True, stop=True)
                ins.then_inc(sem("scores"), 1)

            def into_state(n, bp, q, c):
                a, tk = c // 2, slice(CH * (c % 2), CH * (c % 2) + CH)
                eng.wait_ge(sem("state_kept"), 4 * n + c + 1)
                mm(BST[:, 0:DM], kst[tk, bp, a].rearrange("p h d -> p (h d)"), vpl[tk, bp, a],
                   start=(q == 0 and c == 0), stop=True, skip_group_check=True).then_inc(sem("chunk_in_state"), 1)
                mm(BC[tk, a * DM:(a + 1) * DM], qT[:, bp, c * CH:(c + 1) * CH], sg[:, c % 2], start=True, stop=False, skip_group_check=True)

            def within(n, bp, c):
                a, tk = c // 2, slice(CH * (c % 2), CH * (c % 2) + CH)
                if c == 0:
                    eng.wait_ge(sem("scores_masked"), 4 * (n + 1))
                for pair in range(NH // 2):
                    gp, hh = pair // 4, pair % 4
                    o = (c * 2 + gp) * CH
                    v0 = 2 * DH * pair
                    ins = mm(BC[tk, a * DM + v0:a * DM + v0 + 2 * DH], prob[:, hh, o:o + CH], vexp[:, bp, c, v0:v0 + 2 * DH],
                             start=False, stop=(pair == NH // 2 - 1), skip_group_check=True)
                if c == 3:
                    ins.then_inc(sem("retained"), 1)

            def slot(i, q, prev, back, front, ahead):
                n, m, par, bp, mq = QPS * i + q, QPS * i + q + 1, (q + 1) % 2, q % 2, (q + 1) % QPS
                if back:
                    if due(4 * n):
                        eng.wait_ge(sem("scores_masked"), 4 * n)
                    eng.wait_ge(sem("slots_kept"), 2 * n + 2)
                    for hh in range(4):
                        scores(n, bp, hh)
                if back and not prev:
                    eng.wait_ge(sem("counts_before"), 1)
                    eng.wait_ge(sem("v_kept"), 1)
                    mm(BA[:], T("before"), ra[:].rearrange("p t e -> p (t e)"), start=True, stop=False)
                    mm(BA[:], ones[0:NT, :], cm[:].rearrange("p t e -> p (t e)"), start=False, stop=True).then_inc(sem("rank"), 1)
                if prev:
                    eng.wait_ge(sem("rn_kept"), n)
                    eng.wait_ge(sem("v_kept"), n + 1 if back else n)
                    for a in range(2):
                        ins = eng.transpose(BA[:, a * P:(a + 1) * P], rn[:, a * DM:(a + 1) * DM], ident)
                    ins.then_inc(sem("rn_turned"), 1)
                if back:
                    eng.wait_ge(sem("k_decayed"), n + 1)
                    eng.wait_ge(sem("q_T_kept"), n + 1)
                    eng.wait_ge(sem("v_kept"), n + 1)
                    into_state(n, bp, q, 0)
                if prev:
                    eng.wait_ge(sem("rn_T_kept"), n)
                    for a in range(2):
                        ins = mm(BA[:, a * DM:(a + 1) * DM], rnT[:, a * P:(a + 1) * P], wrow[:, 3, :], start=True, stop=True)
                    ins.then_inc(sem("through_wo"), 1)
                if back:
                    within(n, bp, 0)
                if back:
                    for c in range(1, 4):
                        into_state(n, bp, q, c)
                        within(n, bp, c)
                if front:
                    turn(m, par, 0)
                    for a in range(2):
                        ins = eng.transpose(BS[3][:, a * P:(a + 1) * P], qf[:, par, 0, a * DM:(a + 1) * DM], ident)
                    ins.then_inc(sem("q_turned"), 1)
                    turn(m, par, 1)
                    if ahead:
                        project_qk(i, q + 2)
                    if prev:
                        eng.wait_ge(sem("s_kept"), n)
                    elif back:
                        eng.wait_ge(sem("ranked"), 1)
                    for c in range(4):
                        spread_v(mq, c)
                    for a in range(2):
                        ins = mm(BA[:, 256 + a * DM:256 + (a + 1) * DM], xin[:, mq, a * P:(a + 1) * P], wvc[:], start=True, stop=True)
                    ins.then_inc(sem("v_projected"), 1)

            def body(i):
                for q in range(QPS):
                    slot(i, q, True, True, True, True)

            eng.wait_ge(sem("scales"), 1)
            project_qk(-1, 4)
            slot(-1, 3, False, False, True, True)
            eng.wait_ge(sem("choices"), 1)
            for e in range(NE):
                ins = mm(BST[0:NT, e:e + 1], ra[:, :, e], ones[:, 0:1], start=True, stop=True)
            ins.then_inc(sem("counts"), 1)
            eng.wait_ge(sem("counts_before"), 1)
            mm(BST[:, 0:NE], ones[0:NT, :], cnt[:], start=True, stop=True).then_inc(sem("totals"), 1)
            for q in range(QPS):
                slot(0, q, q > 0, True, True, True)
            with eng.Fori(1, NPAIR // QPS - 1) as i:
                body(i)
            for q in range(QPS):
                slot(NPAIR // QPS - 1, q, True, True, q + 1 < QPS, q + 2 < QPS)
            slot(NPAIR // QPS, 0, True, False, False, False)
            eng.wait_ge(sem("s_kept"), NPAIR)
            eng.wait_ge(sem("slots_kept"), 2 * NPAIR)

            def turn_rows(i, off):
                g, b = EB * i + off, off % EB
                eng.wait_ge(sem(f"rows_read{b}"), 16 * (i + off // EB + 1))
                if due(g):
                    eng.wait_ge(sem("rows_T_kept"), g)
                for s in range(ES):
                    ins = eng.transpose(BST[:, s * P:(s + 1) * P], xr[:, b, s, 0:DM], ident)
                ins.then_inc(sem("rows_turned"), 1)

            def layer1(i, off):
                g, par, b = EB * i + off, off % 2, off % EB
                eng.wait_ge(sem("rows_T_kept"), g + 1)
                eng.wait_ge(sem(f"expert_weights{b}"), 16 * (i + off // EB + 1))
                for c in range(FC):
                    if due(FC * (g - 1) + c + 1):
                        eng.wait_ge(sem("hidden"), FC * (g - 1) + c + 1)
                    mm(BS[c][:, par * ET:(par + 1) * ET], wb[:, b, c * P:(c + 1) * P], xT[:, par], start=True, stop=True).then_inc(sem("layer1"), 1)

            def layer2(i, b):
                g, par, bank = EB * i + b, b % 2, (BA, BB)[b % 2]
                if due(g):
                    eng.wait_ge(sem("biased"), g)
                eng.wait_ge(sem("hidden"), FC * (g + 1))
                for s in range(ES):
                    for c in range(FC):
                        ins = mm(bank[:, s * DM:(s + 1) * DM], hT[:, par, c, s * P:(s + 1) * P],
                                 wb[:, b, W1W + c * DM:W1W + (c + 1) * DM], start=(c == 0), stop=(c == FC - 1))
                ins.then_inc(sem("layer2"), 1)

            turn_rows(0, 0)
            layer1(0, 0)
            turn_rows(0, 1)
            def body(i, ahead=2 * EB):
                for b in range(EB):
                    if b + 1 < ahead:
                        layer1(i, b + 1)
                    if b + 2 < ahead:
                        turn_rows(i, b + 2)
                    layer2(i, b)

            turns(eng, NET // EB - 1, body)
            body(NET // EB - 1, EB)


NAMES = ("x", "WQ", "WK", "WV", "WO", "gamma", "beta")
FFN_NAMES = ("gate_w", "gate_b", "w1", "b1", "w2", "b2")


def kernel(**inputs):
    from concourse import bacc
    from concourse.bass_utils import run_bass_kernel_spmd

    nc = bacc.Bacc("TRN2", target_bir_lowering=False, num_devices=1)
    arrays = {f"in_{n}": np.ascontiguousarray(inputs[f"L0_attn_{n}"]) for n in NAMES}
    arrays.update({f"in_{n}": np.ascontiguousarray(inputs[f"L0_ffn_{n}"]) for n in FFN_NAMES})
    arrays["in_x"] = arrays["in_x"].reshape(TOK, DM)
    arrays["tables"], at = constants()
    args = [nc.dram_tensor(n, a.shape, mybir.dt.from_np(a.dtype), kind="ExternalInput").ap() for n, a in arrays.items()]
    out = nc.dram_tensor("out", (TOK, DM), mybir.dt.float32, kind="ExternalOutput").ap()
    moe_retention(nc, *args, out, at)
    r = run_bass_kernel_spmd(nc, [arrays], core_ids=[0])
    return np.asarray(r.results[0]["out"]).reshape(NSEQ, SEQ, DM)
```
